# Optimizing a Trainium2 kernel written in Bass

```python
import numpy as np
import jax
import jax.numpy as jnp

def _softmax(x, axis=-1):
    return jax.nn.softmax(x, axis=axis)

def _gelu(x):
    return jax.nn.gelu(x, approximate=True)

def _silu(x):
    return jax.nn.silu(x)

def _sigmoid(x):
    return jax.nn.sigmoid(x)

def _layernorm(x, axis=-1, eps=1e-05):
    m = jnp.mean(x, axis=axis, keepdims=True)
    v = jnp.var(x, axis=axis, keepdims=True)
    return (x - m) / jnp.sqrt(v + eps)

def _scatter_add(tgt, idx, src, axis=0):
    return tgt.at[idx].add(src)

def _segment_sum(src, seg, n):
    return jax.ops.segment_sum(src, seg, n)
kernel_name = 'mk_flamingo_gated_d1_seqx_r2_73bf45'

def setup_inputs(seed: int=0):
    np.random.seed(seed)
    _w = jnp.asarray

    def _rec_inputs():
        import jax
        import jax.numpy as jnp
        _rk = jax.random.key(seed)
        x = 7.22e-05 + 1 * jax.random.normal(jax.random.fold_in(_rk, 1), (2, 2048, 512), jnp.float32)
        _lenS = 2048 - jax.random.randint(jax.random.fold_in(_rk, 7), (2,), 0, max(1, 2048 // 4) + 1, jnp.int32)
        _lenS2 = 77 - jax.random.randint(jax.random.fold_in(_rk, 8), (2,), 0, max(1, 77 // 4) + 1, jnp.int32)
        _ctx_768P = jax.random.normal(jax.random.fold_in(_rk, 11), (2, 16, 384), jnp.float32)
        _ctx_768c = jax.random.dirichlet(jax.random.fold_in(_rk, 511), 0.3 * jnp.ones((16,), jnp.float32), (2, 77))
        _ctx_768t = jnp.einsum('bsk,bkd->bsd', _ctx_768c, _ctx_768P)
        _ctx_768t = _ctx_768t * jax.lax.rsqrt(jnp.mean(jnp.square(_ctx_768t)) + 1e-12) * 0.953939
        ctx_768 = -0.000191848 + 0.999787 * (_ctx_768t + 0.3 * jax.random.normal(jax.random.fold_in(_rk, 611), (2, 77, 384), jnp.float32))
        _g = jax.random.normal(jax.random.fold_in(_rk, 9001), (2, 1), jnp.float32)
        _g = jnp.sign(_g) * jnp.maximum(jnp.abs(_g), 1.0) + (_g == 0) * 1.0
        g_xattn = _g[0]
        g_ffn = _g[1]
        return (x, ctx_768, g_xattn, g_ffn)
    x, ctx_768, g_xattn, g_ffn = _rec_inputs()

    def _L0_xattn_setup():
        import jax, jax.numpy as jnp
        import numpy as np
        NUM_HEADS = 16
        CLAMP = 10000.0
        key = jax.random.key(seed)
        ks = jax.random.split(key, 8)
        B, Nq, Nkv, Cq, Ckv = (4, 1024, 1024, 512, 384)
        s_q = 1.0 / np.sqrt(Cq)
        s_kv = 1.0 / np.sqrt(Ckv)
        return {'query': jax.random.normal(ks[0], (B, Nq, Cq), jnp.float32), 'key_value': jax.random.normal(ks[1], (B, Nkv, Ckv), jnp.float32), 'Wq': jax.random.normal(ks[2], (Cq, Cq), jnp.float32) * s_q, 'bq': jnp.zeros((Cq,), jnp.float32), 'Wk': jax.random.normal(ks[3], (Ckv, Cq), jnp.float32) * s_kv, 'bk': jnp.zeros((Cq,), jnp.float32), 'Wv': jax.random.normal(ks[4], (Ckv, Cq), jnp.float32) * s_kv, 'bv': jnp.zeros((Cq,), jnp.float32), 'Wo': jax.random.normal(ks[5], (Cq, Cq), jnp.float32) * s_q, 'bo': jnp.zeros((Cq,), jnp.float32)}
    _L0_xattn_all = _L0_xattn_setup()
    _L0_xattn_in = {k: v for k, v in _L0_xattn_all.items() if k in ('Wq', 'bq', 'Wk', 'bk', 'Wv', 'bv', 'Wo', 'bo')}
    del _L0_xattn_all

    def _L0_ffn_setup():
        import math
        import jax, jax.numpy as jnp
        import numpy as np
        NUM_EXPERTS = 16
        TOP_K = 2
        CAPACITY_FACTOR = 1.25
        key = jax.random.key(seed)
        k1, k2, k3, k4 = jax.random.split(key, 4)
        d, dff, E = (512, 2048, NUM_EXPERTS)
        x = jax.random.normal(k1, (4, 1024, d), dtype=jnp.float32)
        router_w = jax.random.normal(k2, (E, d), dtype=jnp.float32) * d ** (-0.5)
        router_b = jnp.zeros((E,), dtype=jnp.float32)
        w1 = jax.random.normal(k3, (E, d, dff), dtype=jnp.float32) * 0.02
        b1 = jnp.zeros((E, dff), dtype=jnp.float32)
        w2 = jax.random.normal(k4, (E, dff, d), dtype=jnp.float32) * 0.02
        b2 = jnp.zeros((E, d), dtype=jnp.float32)
        return {'x': x, 'router_w': router_w, 'router_b': router_b, 'w1': w1, 'b1': b1, 'w2': w2, 'b2': b2}
    _L0_ffn_all = _L0_ffn_setup()
    _L0_ffn_in = {k: v for k, v in _L0_ffn_all.items() if k in ('router_w', 'router_b', 'w1', 'b1', 'w2', 'b2')}
    del _L0_ffn_all
    return {'x': x, 'ctx_768': ctx_768, 'g_xattn': g_xattn, 'g_ffn': g_ffn, 'L0_xattn_Wq': _L0_xattn_in['Wq'], 'L0_xattn_bq': _L0_xattn_in['bq'], 'L0_xattn_Wk': _L0_xattn_in['Wk'], 'L0_xattn_bk': _L0_xattn_in['bk'], 'L0_xattn_Wv': _L0_xattn_in['Wv'], 'L0_xattn_bv': _L0_xattn_in['bv'], 'L0_xattn_Wo': _L0_xattn_in['Wo'], 'L0_xattn_bo': _L0_xattn_in['bo'], 'L0_ffn_router_w': _L0_ffn_in['router_w'], 'L0_ffn_router_b': _L0_ffn_in['router_b'], 'L0_ffn_w1': _L0_ffn_in['w1'], 'L0_ffn_b1': _L0_ffn_in['b1'], 'L0_ffn_w2': _L0_ffn_in['w2'], 'L0_ffn_b2': _L0_ffn_in['b2']}

def reference(x, ctx_768, g_xattn, g_ffn, L0_xattn_Wq, L0_xattn_bq, L0_xattn_Wk, L0_xattn_bk, L0_xattn_Wv, L0_xattn_bv, L0_xattn_Wo, L0_xattn_bo, L0_ffn_router_w, L0_ffn_router_b, L0_ffn_w1, L0_ffn_b1, L0_ffn_w2, L0_ffn_b2):
    import jax
    import jax.numpy as jnp

    def _L0_xattn_ref(query, key_value, Wq, bq, Wk, bk, Wv, bv, Wo, bo):
        import jax, jax.numpy as jnp
        import numpy as np
        NUM_HEADS = 16
        CLAMP = 10000.0
        B, Nq, Cq = query.shape
        Nkv = key_value.shape[1]
        H = NUM_HEADS
        D = Cq // H
        scale = D ** (-0.5)
        q = (query @ Wq + bq).reshape(B, Nq, H, D).transpose(0, 2, 1, 3)
        k = (key_value @ Wk + bk).reshape(B, Nkv, H, D).transpose(0, 2, 1, 3)
        v = (key_value @ Wv + bv).reshape(B, Nkv, H, D).transpose(0, 2, 1, 3)
        attn = jnp.einsum('bhqd,bhkd->bhqk', q, k) * scale
        attn = jnp.clip(attn, -CLAMP, CLAMP)
        attn = jax.nn.softmax(attn, axis=-1)
        attn = jnp.where(jnp.any(jnp.isnan(attn)), jnp.asarray(1.0 / Nkv, attn.dtype), attn)
        x = jnp.einsum('bhqk,bhkd->bqhd', attn, v).reshape(B, Nq, Cq)
        return x @ Wo + bo

    def _L0_ffn_ref(x, router_w, router_b, w1, b1, w2, b2):
        import math
        import jax, jax.numpy as jnp
        import numpy as np
        NUM_EXPERTS = 16
        TOP_K = 2
        CAPACITY_FACTOR = 1.25
        E, k = (NUM_EXPERTS, TOP_K)
        B, S, d = x.shape
        tokens = B * S
        capacity = max(1, int(math.ceil(CAPACITY_FACTOR * tokens * k / E)))
        x2d = x.reshape(tokens, d)
        logits = x2d @ router_w.T + router_b
        vals, idx = jax.lax.top_k(logits, k)
        gates = jax.nn.softmax(vals, axis=-1)
        flat_e = idx.reshape(-1)
        oh = (flat_e[:, None] == jnp.arange(E)[None, :]).astype(jnp.int32)
        pos = jnp.take_along_axis(jnp.cumsum(oh, axis=0) - 1, flat_e[:, None], axis=1)[:, 0]
        kept = pos < capacity
        kept2 = kept.reshape(tokens, k)
        denom = jnp.sum(gates * kept2, axis=-1, keepdims=True)
        gates = jnp.where(kept2, gates / (denom + 1e-09), 0.0)
        slot = flat_e * capacity + pos
        slot_safe = jnp.where(kept, slot, E * capacity)
        x_rep = jnp.repeat(x2d, k, axis=0)
        buf = jnp.zeros((E * capacity + 1, d), x.dtype).at[slot_safe].set(x_rep)
        packed = buf[:E * capacity].reshape(E, capacity, d)
        h = jax.nn.gelu(jnp.einsum('ecd,edf->ecf', packed, w1) + b1[:, None, :], approximate=False)
        expert_out = jnp.einsum('ecf,efd->ecd', h, w2) + b2[:, None, :]
        eflat = expert_out.reshape(E * capacity, d)
        gathered = eflat[jnp.clip(slot, 0, E * capacity - 1)]
        w = (gates.reshape(-1) * kept.astype(x.dtype))[:, None]
        out = (gathered * w).reshape(tokens, k, d).sum(axis=1)
        return out.reshape(B, S, d)
    x = x + jnp.tanh(g_xattn[0]) * _L0_xattn_ref(_layernorm(x, axis=-1), ctx_768, L0_xattn_Wq, L0_xattn_bq, L0_xattn_Wk, L0_xattn_bk, L0_xattn_Wv, L0_xattn_bv, L0_xattn_Wo, L0_xattn_bo)
    x = x + jnp.tanh(g_ffn[0]) * _L0_ffn_ref(_layernorm(x, axis=-1), L0_ffn_router_w, L0_ffn_router_b, L0_ffn_w1, L0_ffn_b1, L0_ffn_w2, L0_ffn_b2)
    return x

_drawn_inputs = setup_inputs


def setup_inputs(seed=0):
    import zlib

    import numpy as np

    out = dict(_drawn_inputs(seed))
    spreads = {'L0_xattn_bq': (0.0, 0.1),
     'L0_xattn_bk': (0.0, 0.1),
     'L0_xattn_bv': (0.0, 0.1),
     'L0_xattn_bo': (0.0, 0.1),
     'L0_ffn_router_b': (0.0, 0.1),
     'L0_ffn_b1': (0.0, 0.1),
     'L0_ffn_b2': (0.0, 0.1)}
    factors = {}
    for name, (base, spread) in spreads.items():
        noise = np.random.default_rng([zlib.crc32(name.encode()), seed]).standard_normal(out[name].shape)
        drawn = base * np.exp(spread * noise) if base else spread * noise
        out[name] = jnp.asarray(drawn.astype(out[name].dtype))
    for name, factor in factors.items():
        out[name] = (out[name] * factor).astype(out[name].dtype)
    return out
```

```python
from contextlib import ExitStack

import concourse.bass as bass
from concourse import mybir

ALU = mybir.AluOpType
ACT = mybir.ActivationFunctionType
AX = mybir.AxisListType
F32 = mybir.dt.float32
F32R = mybir.dt.float32r
BF16 = mybir.dt.bfloat16
I32 = mybir.dt.int32
P = 128
BANK = 512


class Sem:

    def __init__(self, nc, ctx, name):
        self.sem = ctx.enter_context(nc.semaphore(name))
        self.value = 0

    def up(self, ins, by=1):
        ins.then_inc(self.sem, by)
        self.value += by
        return (self, self.value)

    def dma(self, ins):
        return self.up(ins, 16)


class Buf:

    def __init__(self, ap):
        self.ap = ap
        self.ready = ()
        self.free = ()


def moe_block_kernel(nc, x, ctx_in, g_xattn, g_ffn, Wq, bq, Wk, bk, Wv, bv, Wo, bo,
                     router_w, router_b, w1, b1, w2, b2, out):
    NB, SEQ, D = x.shape
    NKV, CK = ctx_in.shape[1:]
    E, _, FF = w1.shape
    H = 16
    DH = D // H
    TOK = NB * SEQ
    TOPK = 2
    CAP = -(-5 * TOK * TOPK // (4 * E))
    CLAMP = 10000.0
    SCALE = float(DH) ** -0.5
    EPS = 1e-5
    KD = D // P
    KC = CK // P
    NG = D // P
    HG = P // DH
    SUP = BANK
    TPS = SUP // P
    NS = TOK // SUP
    SPB = SEQ // SUP
    KEYS = H * NKV
    NCH = -(-KEYS // P)
    GK = HG * NKV
    HH = H // 2
    NF = FF // P
    ST = CAP // P
    HALF = CAP // 2
    CF = BANK // P
    NC = NF // CF
    NROW = E * ST
    NOBODY = float(TOK)
    FAR = 1.0e6
    assert CAP % P == 0 and HALF <= BANK and KEYS <= NCH * P and NROW <= P and GK <= BANK

    pairs = [[c for c in range(NCH) if c * P < (g + 1) * GK and (c + 1) * P > g * GK] for g in range(NG)]
    pair_at = {}
    for g in range(NG):
        for c in pairs[g]:
            pair_at[c, g] = len(pair_at)

    pe, act, dve, pool, sp = nc.tensor, nc.scalar, nc.vector, nc.gpsimd, nc.sync
    x_rows = x.rearrange("b s d -> (b s) d")
    out_rows = out.rearrange("b s d -> (b s) d")
    x_sup = x_rows.rearrange("(s t p) d -> s p t d", p=P, t=TPS)
    out_sup = out_rows.rearrange("(s t p) d -> s p t d", p=P, t=TPS)
    normed = nc.dram_tensor("normed_rows", (TOK, D), F32).ap()
    normed_sup = normed.rearrange("(s t p) d -> s p t d", p=P, t=TPS)
    table = nc.dram_tensor("slot_table", (E * CAP, 2), F32).ap()

    top = ExitStack()
    with top:
        sems = {}

        def S(name):
            if name not in sems:
                sems[name] = Sem(nc, top, name)
            return sems[name]

        seen = {}

        def wait(eng, *events):
            for event in events:
                if event is None:
                    continue
                if isinstance(event, list) or (event and not isinstance(event[0], Sem)) or event == ():
                    wait(eng, *event)
                    continue
                sem, value = event
                if seen.get((id(eng), id(sem)), 0) < value:
                    seen[id(eng), id(sem)] = value
                    eng.wait_ge(sem.sem, value)

        def sb(ctx, name, shape, dt=F32):
            return ctx.enter_context(nc.sbuf_tensor(name, shape, dt))

        ring_a = [top.enter_context(nc.psum_tensor(f"ring_a{i}", [P, BANK], F32)) for i in range(2)]
        pair = [top.enter_context(nc.psum_tensor(f"pair{i}", [P, 2, BANK], F32)) for i in range(2)]
        ring_b = [top.enter_context(nc.psum_tensor(f"ring_b{i}", [P, BANK], F32)) for i in range(2)]
        bank_a = [Buf(t) for t in ring_a]
        bank_b = [Buf(t) for t in ring_b]
        score_pair = [Buf(t) for t in pair]
        turn = {"a": 0, "b": 0, "s": 0, "m": 0}

        def take(name, banks):
            turn[name] += 1
            return banks[(turn[name] - 1) % len(banks)]

        ident = sb(top, "ident", [P, P])
        ones_f = sb(top, "ones_f", [P, P])
        ones_b = sb(top, "ones_b", [P, P], BF16)
        before = sb(top, "before", [P, P], BF16)
        expert_no = sb(top, "expert_no", [P, E])
        expert_no_far = sb(top, "expert_no_far", [P, E])
        token_no = sb(top, "token_no", [P, TOK // P])
        tanh_g = sb(top, "tanh_g", [P, 2])
        bias_cols = sb(top, "bias_cols", [P, 2 * KD])
        b1_cols = sb(top, "b1_cols", [P, E * NF])
        router_wT = sb(top, "router_wT", [P, KD, E])
        router_b_col = sb(top, "router_b_col", [E, 1])
        bo_rows = sb(top, "bo_rows", [P, D])
        mean_v = sb(top, "mean_v", [P, NG, NB])
        nan_sums = sb(top, "nan_sums", [P, 2 * TOK // P])
        nan_scrap = sb(top, "nan_scrap", [P, 2 * GK], BF16)
        nan_total = sb(top, "nan_total", [P, 1])
        no_nan = sb(top, "no_nan", [P, 1])
        keep_mask = sb(top, "keep_mask", [P, 1], I32)
        drop_mask = sb(top, "drop_mask", [P, 1], I32)
        mean_bits = sb(top, "mean_bits", [P, NG, NB], I32)
        stats = sb(top, "stats", [P, TPS, 6])
        mean_var = sb(top, "mean_var", [P, TPS, 2])
        var_eps = sb(top, "var_eps", [P, TPS])
        half_bits = sb(top, "half_bits", [P, TPS], I32)
        rstd = sb(top, "rstd", [P, TPS])
        newton = sb(top, "newton", [P, TPS])
        NSM = 4
        smax = [sb(top, f"smax{i}", [P, HH]) for i in range(NSM)]
        ssum = [sb(top, f"ssum{i}", [P, HH]) for i in range(NSM)]
        slot_token = sb(top, "slot_token", [P, NROW], I32)
        slot_gate = sb(top, "slot_gate", [P, NROW])

        lay1 = ExitStack()
        Wq_hi = sb(lay1, "Wq_hi", [P, KD, D], F32R)
        Wq_lo = sb(lay1, "Wq_lo", [P, KD, D], F32R)
        k_block = sb(lay1, "k_block", [P, NB, NG, GK])
        v_pack = sb(lay1, "v_pack", [P, NB, len(pair_at), P])
        xT_hi = Buf(sb(lay1, "xT_hi", [P, KD, SUP], F32R))
        xT_lo = Buf(sb(lay1, "xT_lo", [P, KD, SUP], F32R))
        qT = Buf(sb(lay1, "qT", [P, NG, SUP]))
        NP = 3
        probs = [Buf(sb(lay1, f"probs{i}", [P, NCH * P])) for i in range(NP)]
        pT = Buf(sb(lay1, "pT", [P, NCH, SUP]))
        lay12 = ExitStack()
        raw = ExitStack()
        Wq_raw = sb(raw, "Wq_raw", [P, KD, D])
        Wo_raw = sb(raw, "Wo_raw", [P, KD, D])
        Wk_sb = sb(raw, "Wk_sb", [P, KC, D])
        Wv_sb = sb(raw, "Wv_sb", [P, KC, D])
        ctx_sb = sb(raw, "ctx_sb", [NKV, NB, CK])
        ctxT = sb(raw, "ctxT", [P, KC, NB * NKV])
        v_sb = sb(raw, "v_sb", [NKV, NB, D])
        inv_keys = sb(raw, "inv_keys", [P, 1])
        bias_rows = sb(raw, "bias_rows", [2 * KD, P])
        b1_rows = sb(raw, "b1_rows", [P, E * NF // P, P])
        bv_row = sb(raw, "bv_row", [1, D])
        bo_row = sb(raw, "bo_row", [1, D])
        rw_rows = sb(raw, "rw_rows", [E, D])
        gate_in = sb(raw, "gate_in", [P, 2])
        table_init = sb(raw, "table_init", [NROW, P, 2])
        raw.close()
        attn_out = sb(lay12, "attn_out", [P, NG, TOK])
        xs = [Buf(sb(lay12, f"x_sup{i}", [P, TPS, D])) for i in range(2)]
        Wo_hi = sb(lay12, "Wo_hi", [P, KD, D], F32R)
        Wo_lo = sb(lay12, "Wo_lo", [P, KD, D], F32R)
        lay12.close()
        lay1.close()
        lay3 = top
        w_raw = [(Buf(sb(lay3, f"w1_raw{i}", [P, KD, BANK])), Buf(sb(lay3, f"w2_raw{i}", [P, CF, D])))
                 for i in range(2)]
        xg = Buf(sb(lay3, "gathered", [P, ST, D]))
        lay2 = ExitStack()
        ao_hi = Buf(sb(lay2, "ao_hi", [P, NG, SUP], F32R))
        ao_lo = Buf(sb(lay2, "ao_lo", [P, NG, SUP], F32R))
        xn2 = [Buf(sb(lay2, f"xn2_{i}", [P, TPS, D])) for i in range(2)]
        xn2T = Buf(sb(lay2, "xn2T", [P, KD, SUP]))
        logitT = Buf(sb(lay2, "logitT", [E, SUP]))
        logits = sb(lay2, "logits", [P, TPS, E])
        rest = sb(lay2, "rest", [P, TPS, E])
        hit = sb(lay2, "hit", [P, TPS, E])
        place = sb(lay2, "place", [P, TPS, E])
        one_hot = sb(lay2, "one_hot", [P, TOPK, TPS, E])
        chosen = [sb(lay2, f"chosen{i}", [P, TPS, E], BF16) for i in range(2)]
        taken = sb(lay2, "taken", [P, 2, TPS + 1, E], BF16)
        best = sb(lay2, "best", [P, TOPK, TPS])
        best_no = sb(lay2, "best_no", [P, TOPK, TPS])
        prior = sb(lay2, "prior", [P, TOPK, TPS, E])
        pos = sb(lay2, "pos", [P, TOPK, TPS])
        kept = sb(lay2, "kept", [P, TOPK, TPS])
        away = sb(lay2, "away", [P, TOPK, TPS])
        gap = sb(lay2, "gap", [P, TPS])
        gexp = sb(lay2, "gexp", [P, TPS])
        gden = sb(lay2, "gden", [P, TPS])
        gate = sb(lay2, "gate", [P, TOPK, TPS])
        slots = [Buf(sb(lay2, f"slots{i}", [P, TOPK, TPS], I32)) for i in range(2)]
        entry = [Buf(sb(lay2, f"entry{i}", [P, TOPK, TPS, 2])) for i in range(2)]
        table_sb = sb(lay2, "table_sb", [NROW, P, 2])
        lay2.close()
        w_split = [[Buf(sb(lay3, f"{n}_{h}{i}", [P, CF, BANK], F32R)) for n in ("w1", "w2") for h in ("hi", "lo")]
                   for i in range(2)]
        xgT = [(Buf(sb(lay3, f"xgT_hi{i}", [P, KD, CAP], F32R)), Buf(sb(lay3, f"xgT_lo{i}", [P, KD, CAP], F32R)))
               for i in range(2)]
        h_full = [Buf(sb(lay3, f"h_full{i}", [P, HALF])) for i in range(3)]
        NH = 4
        h_hi = [Buf(sb(lay3, f"h_hi{i}", [P, CAP], F32R)) for i in range(NH)]
        h_lo = [Buf(sb(lay3, f"h_lo{i}", [P, CAP], F32R)) for i in range(NH)]
        b2_rows = [Buf(sb(lay3, f"b2_rows{i}", [P, D])) for i in range(2)]
        y = Buf(sb(lay3, "y", [P, ST, D]))

        def row(v):
            return v.rearrange("(a n) -> a n", a=1)

        def bc(ap, shape, dim=None):
            return ap.to_broadcast(shape)

        def load_x(s):
            b = xs[s % NS % 2]
            wait(sp, b.free)
            b.ready = S(f"load_x{s % NS % 2}").dma(sp.dma_start(b.ap[:], x_sup[s % NS]))

        S_small = S("load_small")
        for dst, src in ((ctx_sb[:], ctx_in.rearrange("b j c -> j b c")),
                         (bias_rows[0:KD, :], bq.rearrange("(k p) -> k p", p=P)),
                         (bias_rows[KD:2 * KD, :], bk.rearrange("(k p) -> k p", p=P)),
                         (bv_row[:], row(bv)), (bo_row[:], row(bo)),
                         (rw_rows[:], router_w),
                         (router_b_col[:], router_b.rearrange("(e a) -> e a", a=1)),
                         (gate_in[:, 0:1], g_xattn.partition_broadcast(P)),
                         (gate_in[:, 1:2], g_ffn.partition_broadcast(P)),
                         (b1_rows[:], b1.rearrange("e (f p) -> (e f) p", p=P).rearrange("(r q) p -> q r p", q=P))):
            small = S_small.dma(act.dma_start(dst, src))
        wk_in = S("load_wk").dma(sp.dma_start(Wk_sb[:], Wk.rearrange("(k p) n -> p k n", p=P)))
        wv_in = S("load_wv").dma(sp.dma_start(Wv_sb[:], Wv.rearrange("(k p) n -> p k n", p=P)))
        load_x(0)
        wq_in = S("load_wq").dma(sp.dma_start(Wq_raw[:], Wq.rearrange("(k p) n -> p k n", p=P)))
        load_x(1)
        wo_in = S("load_wo").dma(sp.dma_start(Wo_raw[:], Wo.rearrange("(k p) n -> p k n", p=P)))

        const = S("pool_const")
        const.up(pool.memset(ident[:], 0.0))
        const.up(pool.memset(before[:], 1.0))
        const.up(pool.memset(ones_b[:], 1.0))
        filled = const.up(pool.memset(ones_f[:], 1.0))
        wait(pool, filled)
        const.up(pool.affine_select(out=ident[:], in_=ident[:], compare_op=ALU.not_equal, fill=1.0, base=0,
                                    pattern=[[-1, P]], channel_multiplier=1))
        const.up(pool.affine_select(out=before[:], in_=before[:], compare_op=ALU.is_gt, fill=0.0, base=0,
                                    pattern=[[1, P]], channel_multiplier=-1))
        const.up(pool.iota(expert_no[:], pattern=[[1, E]], base=0, channel_multiplier=0,
                           allow_small_or_imprecise_dtypes=True))
        const.up(pool.iota(expert_no_far[:], pattern=[[1, E]], base=100, channel_multiplier=0,
                           allow_small_or_imprecise_dtypes=True))
        const.up(pool.iota(token_no[:], pattern=[[P, TOK // P]], base=0, channel_multiplier=1,
                           allow_small_or_imprecise_dtypes=True))
        const.up(pool.memset(table_init[:], 0.0))
        const.up(pool.memset(inv_keys[:], 1.0 / NKV))
        for b in range(NP):
            const.up(pool.memset(probs[b].ap[:, KEYS:NCH * P], 0.0))
        const.up(pool.memset(k_block[:], 0.0))
        const.up(pool.memset(v_pack[:], 0.0))
        const_done = const.up(pool.memset(taken[:, 0, 0, :], 0.0))
        wait(pool, const_done)
        init_ids = const.up(pool.memset(table_init[:, :, 0:1], NOBODY))
        wait(sp, init_ids)
        table_clear = S("table_clear").dma(
            sp.dma_start(table.rearrange("(r p) c -> r p c", p=P), table_init[:]))

        wait(act, small)
        tanh_done = S("act_tanh").up(act.activation(tanh_g[:], gate_in[:], ACT.Tanh))

        def evac_copy(eng, dst, src, sem):
            if eng is act:
                return sem.up(act.activation(dst, src, ACT.Copy))
            return sem.up(eng.tensor_copy(dst, src))

        wait(pe, small, const_done)
        setup_pe, setup_dve = S("pe_setup"), S("dve_setup")
        for b in range(NB):
            bank = take("a", bank_a)
            wait(pe, bank.free)
            for k in range(KC):
                ins = pe.transpose(bank.ap[:, k * NKV:(k + 1) * NKV], ctx_sb[:, b, k * P:(k + 1) * P],
                                   ident[0:NKV, 0:NKV])
            wait(dve, setup_pe.up(ins))
            for k in range(KC):
                ctx_turned = setup_dve.up(dve.tensor_copy(ctxT[:, k, b * NKV:(b + 1) * NKV],
                                                          bank.ap[:, k * NKV:(k + 1) * NKV]))
            bank.free = ctx_turned
        bank = take("a", bank_a)
        wait(pe, bank.free)
        pe.transpose(bank.ap[:, 0:2 * KD], bias_rows[:], ident[0:2 * KD, 0:2 * KD])
        for k in range(KD):
            pe.transpose(bank.ap[:, 16 + k * E:16 + (k + 1) * E], rw_rows[:, k * P:(k + 1) * P], ident[0:E, 0:E])
        for r in range(E * NF // P):
            ins = pe.transpose(bank.ap[:, 128 + r * P:128 + (r + 1) * P], b1_rows[:, r, :], ident[:])
        wait(dve, setup_pe.up(ins))
        setup_dve.up(dve.tensor_copy(bias_cols[:], bank.ap[:, 0:2 * KD]))
        setup_dve.up(dve.tensor_copy(router_wT[:].rearrange("p k e -> p (k e)"), bank.ap[:, 16:16 + KD * E]))
        cols_done = setup_dve.up(dve.tensor_copy(b1_cols[:], bank.ap[:, 128:128 + E * NF]))
        bank.free = cols_done
        bank = take("a", bank_a)
        wait(pe, bank.free)
        wait(dve, setup_pe.up(pe.matmul(bank.ap[:], ones_f[0:1, :], bo_row[:], start=True, stop=True)), tanh_done)
        bank.free = setup_dve.up(dve.tensor_scalar(bo_rows[:], bank.ap[:], tanh_g[:, 0:1], None, ALU.mult))
        wait(pe, wk_in, ctx_turned)
        wait(dve, cols_done, const_done)
        for g in range(NG):
            bank = take("a", bank_a)
            wait(pe, bank.free)
            for k in range(KC):
                ins = pe.matmul(bank.ap[:, 0:NB * NKV], Wk_sb[:, k, g * P:(g + 1) * P], ctxT[:, k, :],
                                start=k == 0, stop=k == KC - 1)
            wait(dve, setup_pe.up(ins))
            for b in range(NB):
                for a in range(HG):
                    q = slice(a * DH, (a + 1) * DH)
                    k_done = setup_dve.up(dve.tensor_scalar(
                        k_block[q, b, g, a * NKV:(a + 1) * NKV], bank.ap[q, b * NKV:(b + 1) * NKV],
                        bias_cols[q, KD + g:KD + g + 1], SCALE, ALU.add, ALU.mult))
            bank.free = k_done
        wait(pe, wv_in)
        pack = S("pack_v")
        wait(act, const_done)
        for b in range(NB):
            bank = take("a", bank_a)
            wait(pe, bank.free)
            for k in range(KC):
                pe.matmul(bank.ap[0:NKV, :], ctxT[:, k, b * NKV:(b + 1) * NKV], Wv_sb[:, k, :], start=k == 0,
                          stop=False)
            ins = pe.matmul(bank.ap[0:NKV, :], ones_f[0:1, 0:NKV], bv_row[:], start=False, stop=True)
            wait(dve, setup_pe.up(ins))
            v_done = setup_dve.up(dve.tensor_copy(v_sb[:, b, :], bank.ap[0:NKV, :]))
            bank.free = v_done
            wait(sp, v_done, const_done)
            for h in range(H):
                g = h // HG
                for c in pairs[g]:
                    lo, hi = max(h * NKV, c * P), min((h + 1) * NKV, (c + 1) * P)
                    if lo < hi:
                        packed = pack.dma(sp.dma_start(
                            v_pack[lo - c * P:hi - c * P, b, pair_at[c, g], (h % HG) * DH:(h % HG + 1) * DH],
                            v_sb[lo - h * NKV:hi - h * NKV, b, h * DH:(h + 1) * DH]))
        bank = take("a", bank_a)
        wait(pe, bank.free, v_done)
        for g in range(NG):
            for b in range(NB):
                ins = pe.matmul(bank.ap[:, g * NB + b:g * NB + b + 1], v_sb[:, b, g * P:(g + 1) * P],
                                inv_keys[0:NKV, :], start=True, stop=True)
        wait(dve, setup_pe.up(ins))
        mean_done = setup_dve.up(dve.tensor_copy(mean_v[:].rearrange("p g b -> p (g b)"), bank.ap[:, 0:NG * NB]))
        bank.free = mean_done
        wait(act, wq_in)
        wq_hi_done = S("act_wsplit").up(act.activation(Wq_hi[:], Wq_raw[:], ACT.Copy))
        wait(dve, wq_in, wq_hi_done)
        wq_done = setup_dve.up(dve.tensor_tensor(Wq_lo[:], Wq_raw[:], Wq_hi[:], ALU.subtract))

        def split_wo():
            wait(act, wo_in)
            hi = S("act_wsplit").up(act.activation(Wo_hi[:], Wo_raw[:], ACT.Copy))
            wait(pool, wo_in, hi)
            return S("pool_wo").up(pool.tensor_tensor(Wo_lo[:], Wo_raw[:], Wo_hi[:], ALU.subtract))

        ln = S("dve_ln")

        def step(ins):
            wait(dve, ln.up(ins))

        def row_stats(src):
            for t in range(TPS):
                ln.up(dve.bn_stats(stats[:, t, :], src[:, t, :]))
            wait(dve, (ln, ln.value))
            for t in range(TPS):
                ln.up(dve.bn_aggr(mean_var[:, t, :], stats[:, t, :]))
            wait(dve, (ln, ln.value))
            step(dve.tensor_scalar(var_eps[:], mean_var[:, :, 1:2].rearrange("p t a -> p (t a)"), EPS, None, ALU.add))
            step(dve.tensor_scalar(half_bits[:], var_eps[:].bitcast(I32), 1, None, ALU.logical_shift_right))
            step(dve.tensor_scalar(rstd[:].bitcast(I32), half_bits[:], -1.0, float(0x5F3759DF), ALU.mult, ALU.add))
            for _ in range(4):
                step(dve.tensor_tensor(newton[:], rstd[:], rstd[:], ALU.mult))
                step(dve.tensor_tensor(newton[:], newton[:], var_eps[:], ALU.mult))
                step(dve.tensor_scalar(newton[:], newton[:], -0.5, 1.5, ALU.mult, ALU.add))
                step(dve.tensor_tensor(rstd[:], rstd[:], newton[:], ALU.mult))

        def normalise(dst, src):
            for t in range(TPS):
                done = ln.up(dve.tensor_scalar(dst[:, t, :], src[:, t, :], mean_var[:, t, 0:1], rstd[:, t:t + 1],
                                               ALU.subtract, ALU.mult))
            return done

        def norm_x(s):
            b = xs[s % 2]
            wait(dve, b.ready)
            row_stats(b.ap)
            b.ready = normalise(b.ap, b.ap)

        def turn_x(s, k):
            b = xs[s % 2]
            bank = take("a", bank_a)
            wait(pe, bank.free, b.ready)
            for t in range(TPS):
                ins = pe.transpose(bank.ap[:, t * P:(t + 1) * P], b.ap[:, t, k * P:(k + 1) * P], ident[:])
            turned = S("pe_turn_x").up(ins)
            wait(act, turned, xT_hi.free)
            hi = S("act_xT").up(act.activation(xT_hi.ap[:, k, :], bank.ap[:], ACT.Copy))
            wait(dve, turned, hi, xT_lo.free)
            lo = S("dve_xT").up(dve.tensor_tensor(xT_lo.ap[:, k, :], bank.ap[:], xT_hi.ap[:, k, :], ALU.subtract))
            bank.free = (hi, lo)
            xT_hi.ready, xT_lo.ready = hi, lo
            if k == KD - 1:
                b.free = turned

        def split_products(acc, ks, w_hi, w_lo, m_hi, m_lo, first=True, last=True):
            ins = None
            for i, k in enumerate(ks):
                for j, (w, m) in enumerate(((w_hi, m_lo), (w_lo, m_hi), (w_hi, m_hi))):
                    ins = pe.matmul(acc, w(k), m(k), start=first and i == 0 and j == 0,
                                    stop=last and i == len(ks) - 1 and j == 2)
            return ins

        def project_q(s, g):
            bank = take("a", bank_a)
            wait(pe, bank.free, xT_hi.ready, xT_lo.ready, wq_done)
            c = slice(g * P, (g + 1) * P)
            ins = split_products(bank.ap[:], range(KD), lambda k: Wq_hi[:, k, c], lambda k: Wq_lo[:, k, c],
                                 lambda k: xT_hi.ap[:, k, :], lambda k: xT_lo.ap[:, k, :])
            q_done = S("pe_q").up(ins)
            if g == NG - 1:
                xT_hi.free = xT_lo.free = q_done
            wait(act, q_done, qT.free, cols_done)
            bank.free = S("act_q").up(act.activation(qT.ap[:, g, :], bank.ap[:], ACT.Identity,
                                                     bias=bias_cols[:, g:g + 1]))
            qT.ready = bank.free

        softmax = {}

        def scores(u):
            tile, half = divmod(u, 2)
            s, t = divmod(tile, TPS)
            b = s // SPB
            pr = probs[tile % NP]
            sc = take("s", score_pair)
            wait(pe, sc.free, qT.ready, k_done)
            for j in range(2):
                ins = pe.matmul(sc.ap[:, j, 0:GK], qT.ap[:, 2 * half + j, t * P:(t + 1) * P],
                                k_block[:, b, 2 * half + j, :], start=True, stop=True)
            scored = S("pe_scores").up(ins)
            if u % (2 * TPS) == 2 * TPS - 1:
                qT.free = scored
            sc3 = sc.ap[:, :, 0:GK].rearrange("p j (a n) -> p j a n", n=NKV)
            i = u % NSM
            n = S("dve_softmax")
            wait(act, scored, nan_scrap_free[0])
            nan_seen = S("act_nan").up(act.activation(nan_scrap[:].rearrange("p (j n) -> p j n", j=2),
                                                      sc.ap[:, :, 0:GK], ACT.Tanh,
                                                      accum_out=nan_sums[:, u:u + 1]))
            nan_scrap_free[0] = nan_seen
            mx = smax[i]
            wait(dve, nan_seen, pr.free)
            d = pr.ap[:, half * HH * NKV:(half + 1) * HH * NKV]
            clipped = n.up(dve.tensor_scalar(d.rearrange("p (j a n) -> p j a n", j=2, n=NKV), sc3, -CLAMP, CLAMP,
                                             ALU.max, ALU.min))
            wait(dve, clipped, softmax.get(u - NSM, {}).get("all"))
            d3 = d.rearrange("p (a n) -> p a n", n=NKV)
            greatest = n.up(dve.tensor_reduce(mx[:], d3, AX.X, ALU.max))
            sc.free = clipped
            wait(pool, greatest)
            mxb = mx[:].rearrange("p (a o) -> p a o", o=1).to_broadcast([P, HH, NKV])
            softmax[u] = {"less": S("pool_less").up(pool.tensor_tensor(d3, d3, mxb, ALU.subtract))}

        def normal_probs(u):
            tile, half = divmod(u, 2)
            pr = probs[tile % NP]
            d = pr.ap[:, half * HH * NKV:(half + 1) * HH * NKV]
            d3 = d.rearrange("p (a n) -> p a n", n=NKV)
            sm = ssum[u % NSM]
            wait(act, softmax[u]["less"])
            e = S("act_exp").up(act.activation(d, d, ACT.Exp))
            wait(dve, e)
            n = S("dve_softmax")
            wait(dve, n.up(dve.tensor_reduce(sm[:], d3, AX.X, ALU.add)))
            r = n.up(dve.reciprocal(sm[:], sm[:]))
            wait(pool, r, e)
            smb = sm[:].rearrange("p (a o) -> p a o", o=1).to_broadcast([P, HH, NKV])
            pr.ready = S("pool_probs").up(pool.tensor_tensor(d3, d3, smb, ALU.mult))
            softmax[u]["all"] = (pr.ready, r)

        def turn_probs(tile):
            s, t = divmod(tile, TPS)
            pr = probs[tile % NP]
            for n, c0 in enumerate(range(0, NCH, 4)):
                cs = range(c0, min(c0 + 4, NCH))
                bank = take("b", bank_b)
                wait(pe, bank.free, pr.ready)
                for c in cs:
                    ins = pe.transpose(bank.ap[:, (c - c0) * P:(c - c0 + 1) * P], pr.ap[:, c * P:(c + 1) * P], ident[:])
                turned = S("pe_turn_p").up(ins)
                eng = act if n == 1 else dve
                wait(eng, turned, pT.free)
                bank.free = evac_copy(eng, pT.ap[:, cs[0]:cs[-1] + 1, t * P:(t + 1) * P],
                                      bank.ap[:, 0:len(cs) * P].rearrange("p (c n) -> p c n", n=P),
                                      S("act_pT" if eng is act else "dve_pT"))
                pT.ready = (pT.ready, bank.free)
            pr.free = turned

        def attend(s):
            b = s // SPB
            for g in range(NG):
                bank = take("a", bank_a)
                wait(pe, bank.free, pT.ready, packed)
                for c in pairs[g]:
                    ins = pe.matmul(bank.ap[:], v_pack[:, b, pair_at[c, g], :], pT.ap[:, c, :],
                                    start=c == pairs[g][0], stop=c == pairs[g][-1])
                done = S("pe_attend").up(ins)
                wait(act, done, raw_free)
                bank.free = S("act_attn").up(act.activation(attn_out[:, g, s * SUP:(s + 1) * SUP], bank.ap[:],
                                                            ACT.Copy))
            pT.ready = ()
            pT.free = done
            return bank.free

        nan_scrap_free = [None]
        norm_x(0)
        wo_done = split_wo()
        raw_free = (wq_done, wo_done, packed, mean_done, table_clear)
        for k in range(KD):
            turn_x(0, k)
        for g in range(NG):
            project_q(0, g)
        load_x(2)
        units = 2 * TPS * NS
        for u in range(units + 5):
            if u < units:
                s, r = divmod(u, 2 * TPS)
                scores(u)
                if s + 1 < NS:
                    if r == 1:
                        norm_x(s + 1)
                    if 3 <= r < 3 + KD:
                        turn_x(s + 1, r - 3)
            if 1 <= u <= units:
                normal_probs(u - 1)
            if u < units and r == 2 * TPS - 1 and s + 1 < NS:
                if s + 3 <= NS + 1:
                    load_x(s + 3)
                for g in range(NG):
                    project_q(s + 1, g)
            if u >= 5 and (u - 5) % 2 == 0:
                tile = (u - 5) // 2
                turn_probs(tile)
                if tile % TPS == TPS - 1:
                    attn_done = attend(tile // TPS)

        guard = S("dve_guard")
        wait(dve, nan_scrap_free[0])
        wait(pe, guard.up(dve.tensor_reduce(nan_total[:], nan_sums[:], AX.X, ALU.add)))
        bank = take("a", bank_a)
        wait(pe, bank.free)
        summed = S("pe_guard").up(pe.matmul(bank.ap[:, 0:1], ones_f[:], nan_total[:], start=True, stop=True))
        wait(dve, summed)
        wait(dve, guard.up(dve.tensor_copy(nan_total[:], bank.ap[:, 0:1])))
        bank.free = (guard, guard.value)
        wait(dve, guard.up(dve.tensor_tensor(no_nan[:], nan_total[:], nan_total[:], ALU.is_equal)))
        guard.up(dve.tensor_scalar(drop_mask[:], no_nan[:], 1.0, None, ALU.subtract))
        wait(dve, guard.up(dve.tensor_scalar(keep_mask[:], no_nan[:], -1.0, None, ALU.mult)))
        wait(dve, guard.up(dve.tensor_tensor(mean_bits[:].rearrange("p g b -> p (g b)"),
                                             mean_v[:].bitcast(I32).rearrange("p g b -> p (g b)"),
                                             drop_mask[:].to_broadcast([P, NG * NB]), ALU.bitwise_and)))

        route = S("dve_route")
        stored = S("store_out")
        stored_norm = [S("store_normed0"), S("store_normed1")]
        scattered = [S("scatter_table0"), S("scatter_table1")]
        wait(dve, attn_done)
        route.up(dve.memset(taken[:, 0, 0, :], 0.0))

        def r(ins):
            ev = route.up(ins)
            wait(dve, ev)
            return ev

        def guard_split(s):
            b = s // SPB
            sl = slice(s * SUP, (s + 1) * SUP)
            wait(dve, attn_done)
            for g in range(NG):
                bits = attn_out[:, g, sl].bitcast(I32)
                ok = guard.up(dve.tensor_scalar(bits, bits, keep_mask[:, 0:1], mean_bits[:, g, b:b + 1],
                                                ALU.bitwise_and, ALU.bitwise_or))
            wait(act, ok, ao_hi.free)
            ao_hi.ready = S("act_ao").up(act.activation(ao_hi.ap[:], attn_out[:, :, sl], ACT.Copy))
            wait(dve, ok, ao_hi.ready, ao_lo.free)
            ao_lo.ready = S("dve_ao").up(dve.tensor_tensor(ao_lo.ap[:], attn_out[:, :, sl], ao_hi.ap[:], ALU.subtract))

        def residual(s):
            b = xs[s % 2]
            wait(pool, b.ready, wo_done)
            based = S("pool_base").up(pool.tensor_tensor(
                b.ap[:], b.ap[:], bo_rows[:].rearrange("p (o d) -> p o d", o=1).to_broadcast([P, TPS, D]), ALU.add))
            for t in range(TPS):
                bank = take("a", bank_a)
                wait(pe, bank.free, ao_hi.ready, ao_lo.ready)
                tl = slice(t * P, (t + 1) * P)
                ins = split_products(bank.ap[:], range(KD), lambda k: ao_hi.ap[:, k, tl], lambda k: ao_lo.ap[:, k, tl],
                                     lambda k: Wo_hi[:, k, :], lambda k: Wo_lo[:, k, :])
                y_done = S("pe_y").up(ins)
                wait(dve, y_done, based)
                added = S("dve_resid").up(dve.scalar_tensor_tensor(
                    out=b.ap[:, t, :], in0=bank.ap[:], scalar=tanh_g[:, 0:1], in1=b.ap[:, t, :], op0=ALU.mult,
                    op1=ALU.add))
                bank.free = added
            ao_hi.free = ao_lo.free = y_done
            b.ready = added
            wait(sp, added)
            b.free = (stored.dma(sp.dma_start(out_sup[s], b.ap[:])),)

        def norm_rows(s):
            b, n = xs[s % 2], xn2[s % 2]
            wait(dve, b.ready)
            row_stats(b.ap)
            wait(dve, n.free)
            n.ready = normalise(n.ap, b.ap)
            b.free = (*b.free, n.ready)
            wait(sp, n.ready)
            n.free = (stored_norm[s % 2].dma(sp.dma_start(normed_sup[s], n.ap[:])),)

        def router(s):
            n = xn2[s % 2]
            for k in range(KD):
                bank = take("b", bank_b)
                wait(pe, bank.free, n.ready)
                for t in range(TPS):
                    ins = pe.transpose(bank.ap[:, t * P:(t + 1) * P], n.ap[:, t, k * P:(k + 1) * P], ident[:])
                turned = S("pe_turn_n").up(ins)
                eng = act if k % 2 else dve
                wait(eng, turned, xn2T.free)
                bank.free = evac_copy(eng, xn2T.ap[:, k, :], bank.ap[:], S("act_nT" if eng is act else "dve_nT"))
                xn2T.ready = (xn2T.ready, bank.free)
            n.free = (*n.free, turned)
            sc = take("s", score_pair)
            wait(pe, sc.free, xn2T.ready)
            xn2T.ready = ()
            for k in range(KD):
                ins = pe.matmul(sc.ap[0:E, 0, :], router_wT[:, k, :], xn2T.ap[:, k, :], start=k == 0, stop=k == KD - 1)
            xn2T.free = S("pe_router").up(ins)
            wait(act, xn2T.free, logitT.free)
            logitT.ready = S("act_logit").up(act.activation(logitT.ap[:], sc.ap[0:E, 0, :], ACT.Identity,
                                                            bias=router_b_col[:]))
            wait(pe, logitT.ready)
            for t in range(TPS):
                ins = pe.transpose(sc.ap[:, 1, t * E:(t + 1) * E], logitT.ap[:, t * P:(t + 1) * P], ident[0:E, 0:E])
            logitT.free = S("pe_router").up(ins)
            wait(dve, logitT.free)
            r(dve.tensor_copy(logits[:].rearrange("p t e -> p (t e)"), sc.ap[:, 1, 0:TPS * E]))
            sc.free = (route, route.value)

        def over_e(ap):
            return ap.rearrange("p (t o) -> p t o", o=1).to_broadcast([P, TPS, E])

        def over_t(ap):
            return ap.rearrange("p (o e) -> p o e", o=1).to_broadcast([P, TPS, E])

        def top_two(s):
            for k, src in enumerate((logits, rest)):
                r(dve.tensor_reduce(best[:, k, :], src[:], AX.X, ALU.max))
                r(dve.tensor_tensor(hit[:], src[:], over_e(best[:, k, :]), ALU.is_equal))
                r(dve.scalar_tensor_tensor(out=place[:], in0=hit[:], scalar=-100.0, in1=over_t(expert_no_far[:]),
                                           op0=ALU.mult, op1=ALU.add))
                r(dve.tensor_reduce(best_no[:, k, :], place[:], AX.X, ALU.min))
                r(dve.tensor_tensor(one_hot[:, k, :, :], over_t(expert_no[:]), over_e(best_no[:, k, :]), ALU.is_equal))
                if k == 0:
                    r(dve.scalar_tensor_tensor(out=rest[:], in0=one_hot[:, 0, :, :], scalar=-3.0e38, in1=logits[:],
                                               op0=ALU.mult, op1=ALU.add))
            ch, tk = chosen[s % 2], taken[:, s % 2, :, :]
            r(dve.tensor_tensor(ch[:], one_hot[:, 0, :, :], one_hot[:, 1, :, :], ALU.add))
            for t in range(TPS):
                r(dve.tensor_tensor(tk[:, t + 1, :], tk[:, t, :], ch[:, t, :], ALU.add))
            summed = r(dve.tensor_copy(taken[:, (s + 1) % 2, 0, :], tk[:, TPS, :]))
            sc = take("s", score_pair)
            wait(pe, sc.free, summed)
            acc = sc.ap[:, 0, 0:TPS * E]
            pe.matmul(acc, before[:], ch[:].rearrange("p t e -> p (t e)"), start=True, stop=False)
            ins = pe.matmul(acc, ones_b[:], tk[:, 0:TPS, :].rearrange("p t e -> p (t e)"), start=False, stop=True)
            counted = S("pe_count").up(ins)
            return sc, counted

        def place_tokens(s, sc, counted):
            sl, en = slots[s % 2], entry[s % 2]
            r(dve.tensor_tensor(gap[:], best[:, 1, :], best[:, 0, :], ALU.subtract))
            wait(act, (route, route.value))
            wait(dve, S("act_gate").up(act.activation(gexp[:], gap[:], ACT.Exp)))
            r(dve.tensor_scalar(gden[:], gexp[:], 1.0, None, ALU.add))
            r(dve.reciprocal(gate[:, 0, :], gden[:]))
            r(dve.tensor_tensor(gate[:, 1, :], gexp[:], gate[:, 0, :], ALU.mult))
            wait(dve, counted)
            for k in range(TOPK):
                r(dve.tensor_tensor(prior[:, k, :, :], sc.ap[:, 0, 0:TPS * E].rearrange("p (t e) -> p t e", e=E),
                                    one_hot[:, k, :, :], ALU.mult))
            sc.free = (route, route.value)
            r(dve.tensor_reduce(pos[:], prior[:], AX.X, ALU.add))
            r(dve.tensor_scalar(kept[:], pos[:], float(CAP), None, ALU.is_lt))
            r(dve.tensor_scalar(away[:], kept[:], -FAR, FAR, ALU.mult, ALU.add))
            r(dve.tensor_tensor(pos[:], pos[:], away[:], ALU.add))
            wait(dve, sl.free, en.free)
            slot_ok = r(dve.scalar_tensor_tensor(out=sl.ap[:], in0=best_no[:], scalar=float(CAP), in1=pos[:],
                                                 op0=ALU.mult, op1=ALU.add))
            r(dve.tensor_tensor(gate[:], gate[:], kept[:], ALU.mult))
            r(dve.tensor_tensor(gden[:], gate[:, 0, :], gate[:, 1, :], ALU.add))
            r(dve.tensor_scalar(gden[:], gden[:], 1e-9, None, ALU.add))
            r(dve.reciprocal(gden[:], gden[:]))
            r(dve.tensor_scalar(gden[:], gden[:], tanh_g[:, 1:2], None, ALU.mult))
            for k in range(TOPK):
                r(dve.tensor_tensor(en.ap[:, k, :, 1], gate[:, k, :], gden[:], ALU.mult))
                en_ok = r(dve.tensor_copy(en.ap[:, k, :, 0], token_no[:, s * TPS:(s + 1) * TPS]))
            wait(pool, slot_ok, en_ok, table_clear)
            for t in range(TPS):
                for k in range(TOPK):
                    sent = scattered[s % 2].dma(pool.indirect_dma_start(
                        table, bass.IndirectOffsetOnAxis(ap=sl.ap[:, k, t:t + 1], axis=0), en.ap[:, k, t, :], None,
                        bounds_check=E * CAP - 1, oob_is_err=False))
            sl.free = en.free = sent

        def load_chunk(n):
            e, c = divmod(n, NC)
            for i, (buf, src) in enumerate(zip(w_raw[n % 2], (
                    w1[e].rearrange("(k p) f -> p k f", p=P)[:, :, c * BANK:(c + 1) * BANK],
                    w2[e].rearrange("(f p) d -> p f d", p=P)[:, c * CF:(c + 1) * CF, :]))):
                wait(sp, buf.free)
                buf.ready = S(f"load_w{i + 1}_{n % 2}").dma(sp.dma_start(buf.ap[:], src))

        def split_chunk(n, i):
            src, hi, lo = w_raw[n % 2][i], w_split[n % 2][2 * i], w_split[n % 2][2 * i + 1]
            eng, name = (act, "act_whi") if i == 0 else (pool, "pool_whi")
            wait(eng, src.ready, hi.free, stage2_done)
            hi.ready = evac_copy(eng, hi.ap[:], src.ap[:], S(name))
            wait(dve, src.ready, hi.ready, lo.free, stage2_done)
            lo.ready = S("dve_wlo").up(dve.tensor_tensor(lo.ap[:], src.ap[:], hi.ap[:], ALU.subtract))
            src.free = (hi.ready, lo.ready)

        for b in (ao_hi, ao_lo, xn2[0], xn2[1], xn2T, logitT, slots[0], slots[1], entry[0], entry[1]):
            b.free = (attn_done, b.free)
        for b in (*w_raw[0], *w_raw[1]):
            b.free = attn_done
        for s in range(NS + 1):
            if s < NS:
                guard_split(s)
                residual(s)
            if s > 0:
                router(s - 1)
                sc, counted = top_two(s - 1)
            if s < NS:
                norm_rows(s)
                if s + 2 < NS:
                    load_x(s + 2)
            if s > 0:
                place_tokens(s - 1, sc, counted)
            if s == NS - 2:
                load_chunk(0)
                load_chunk(1)

        table_written = ((scattered[0], scattered[0].value), (scattered[1], scattered[1].value))
        out_written = (stored, stored.value)
        normed_written = tuple((q, q.value) for q in stored_norm)
        wait(sp, *table_written)
        table_in = S("load_table").dma(sp.dma_start(table_sb[:], table.rearrange("(r p) c -> r p c", p=P)))
        bank = take("a", bank_a)
        wait(pe, bank.free, table_in)
        for c in range(2):
            ins = pe.transpose(bank.ap[:, c * P:c * P + NROW], table_sb[:, :, c], ident[0:NROW, 0:NROW])
        tables_turned = S("pe_table").up(ins)
        wait(dve, tables_turned)
        r(dve.tensor_copy(slot_token[:], bank.ap[:, 0:NROW]))
        table_done = r(dve.tensor_copy(slot_gate[:], bank.ap[:, P:P + NROW]))
        bank.free = table_done
        stage2_done = (table_done, out_written, *normed_written)

        all_banks = [Buf(ring_a[0]), Buf(ring_a[1]), Buf(pair[0][:, 0, :]), Buf(pair[0][:, 1, :]),
                     Buf(pair[1][:, 0, :]), Buf(pair[1][:, 1, :]), Buf(ring_b[0]), Buf(ring_b[1])]
        for n, old in enumerate((bank_a[0], bank_a[1], score_pair[0], score_pair[0], score_pair[1], score_pair[1],
                                 bank_b[0], bank_b[1])):
            all_banks[n].free = old.free
        y_banks, m_banks = all_banks[:ST], all_banks[ST:]

        wait(pool, attn_done)
        cleared = S("pool_clear").up(pool.memset(xg.ap[:], 0.0))
        wait(pool, cleared)

        def gather(e):
            wait(pool, table_done, *normed_written, xg.free)
            for t in range(ST):
                i = e * ST + t
                xg.ready = S("gather").dma(pool.indirect_dma_start(
                    xg.ap[:, t, :], None, normed, bass.IndirectOffsetOnAxis(ap=slot_token[:, i:i + 1], axis=0),
                    bounds_check=TOK - 1, oob_is_err=False))

        def load_b2(e):
            b = b2_rows[e % 2]
            wait(sp, b.free, stage2_done)
            b.ready = S(f"load_b2_{e % 2}").dma(sp.dma_start(b.ap[:], b2[e].partition_broadcast(P)))

        def turn_rows(e, t):
            hi_b, lo_b = xgT[e % 2]
            bank = take("m", m_banks)
            wait(pe, bank.free, xg.ready)
            for k in range(KD):
                ins = pe.transpose(bank.ap[:, k * P:(k + 1) * P], xg.ap[:, t, k * P:(k + 1) * P], ident[:])
            turned = S("pe_turn_g").up(ins)
            sl = slice(t * P, (t + 1) * P)
            src = bank.ap[:, :].rearrange("p (k n) -> p k n", n=P)
            wait(act, turned, hi_b.free, stage2_done)
            hi = S("act_gT").up(act.activation(hi_b.ap[:, :, sl], src, ACT.Copy))
            wait(dve, turned, hi, lo_b.free, stage2_done)
            lo = S("dve_gT").up(dve.tensor_tensor(lo_b.ap[:, :, sl], src, hi_b.ap[:, :, sl], ALU.subtract))
            bank.free = (hi, lo)
            hi_b.ready, lo_b.ready = hi, lo
            if t == ST - 1:
                xg.free = turned

        def hidden(q, half):
            e, f = divmod(q, NF)
            n, j = divmod(q, CF)
            w_hi, w_lo = w_split[n % 2][0], w_split[n % 2][1]
            x_hi, x_lo = xgT[e % 2]
            bank = take("m", m_banks)
            wait(pe, bank.free, x_hi.ready, x_lo.ready, w_hi.ready, w_lo.ready)
            sl = slice(half * HALF, (half + 1) * HALF)
            c = slice(j * P, (j + 1) * P)
            ins = split_products(bank.ap[:, 0:HALF], range(KD), lambda k: w_hi.ap[:, k, c], lambda k: w_lo.ap[:, k, c],
                                 lambda k: x_hi.ap[:, k, sl], lambda k: x_lo.ap[:, k, sl])
            done = S("pe_hidden").up(ins)
            if half == 1:
                if j == CF - 1:
                    w_hi.free = w_lo.free = done
                if f == NF - 1:
                    x_hi.free = x_lo.free = done
            hh, hl, hf = h_hi[q % NH], h_lo[q % NH], h_full[(2 * q + half) % len(h_full)]
            bias = b1_cols[:, q:q + 1]
            wait(act, done, hf.free, stage2_done)
            full = S("act_gelu").up(act.activation(hf.ap[:], bank.ap[:, 0:HALF], ACT.Gelu, bias=bias))
            wait(act, hh.free)
            hi = S("act_gelu").up(act.activation(hh.ap[:, sl], bank.ap[:, 0:HALF], ACT.Gelu, bias=bias))
            bank.free = hi
            wait(dve, full, hi, hl.free, stage2_done)
            lo = S("dve_hlo").up(dve.tensor_tensor(hl.ap[:, sl], hf.ap[:], hh.ap[:, sl], ALU.subtract))
            hf.free = lo
            hh.ready, hl.ready = hi, lo

        def start_y(e):
            b = b2_rows[e % 2]
            wait(dve, b.ready, y.free, stage2_done)
            for t in range(ST):
                i = e * ST + t
                y.ready = S("dve_y").up(dve.tensor_scalar(y.ap[:, t, :], b.ap[:], slot_gate[:, i:i + 1], None, ALU.mult))
            b.free = y.ready

        def down(q):
            e, f = divmod(q, NF)
            n, j = divmod(q, CF)
            w_hi, w_lo = w_split[n % 2][2], w_split[n % 2][3]
            hh, hl = h_hi[q % NH], h_lo[q % NH]
            for t in range(ST):
                bank = y_banks[t]
                sl = slice(t * P, (t + 1) * P)
                wait(pe, hh.ready, hl.ready, w_hi.ready, w_lo.ready, bank.free if f == 0 else None)
                ins = split_products(bank.ap[:, :], [j], lambda k: hh.ap[:, sl], lambda k: hl.ap[:, sl],
                                     lambda k: w_hi.ap[:, k, :], lambda k: w_lo.ap[:, k, :],
                                     first=f == 0, last=f == NF - 1)
                if f == NF - 1:
                    finish_y(e, t, bank, S("pe_down").up(ins))
            done = S("pe_down").up(ins) if f < NF - 1 else (S("pe_down"), S("pe_down").value)
            hh.free = hl.free = done
            if j == CF - 1:
                w_hi.free = w_lo.free = done

        def finish_y(e, t, bank, product):
            i = e * ST + t
            wait(dve, product, y.ready)
            bank.free = S("dve_yout").up(dve.scalar_tensor_tensor(
                out=y.ap[:, t, :], in0=bank.ap[:, :], scalar=slot_gate[:, i:i + 1], in1=y.ap[:, t, :], op0=ALU.mult,
                op1=ALU.add))
            wait(pool, bank.free, out_written, landed[e - 1] if e else None)
            landed[e] = S("scatter_out").dma(pool.indirect_dma_start(
                out_rows, bass.IndirectOffsetOnAxis(ap=slot_token[:, i:i + 1], axis=0), y.ap[:, t, :], None,
                bounds_check=TOK - 1, oob_is_err=False, compute_op=ALU.add))
            y.free = landed[e]

        landed = {}
        LAG = 2
        gather(0)
        load_b2(0)
        split_chunk(0, 0)
        for t in range(ST):
            turn_rows(0, t)
        split_chunk(0, 1)
        total = E * NF
        for q in range(total + LAG):
            if q < total:
                e, f = divmod(q, NF)
                n, j = divmod(q, CF)
                if e + 1 < E:
                    if f == 2:
                        gather(e + 1)
                        load_b2(e + 1)
                    if 8 <= f < 8 + ST:
                        turn_rows(e + 1, f - 8)
                if f == 5:
                    start_y(e)
                hidden(q, 0)
                hidden(q, 1)
                if n + 1 < E * NC:
                    if j == CF - 2:
                        split_chunk(n + 1, 0)
                    if j == CF - 1:
                        split_chunk(n + 1, 1)
                        if n + 3 < E * NC + 1:
                            load_chunk(n + 2) if n + 2 < E * NC else None
            if q >= LAG:
                down(q - LAG)
        wait(sp, out_written, *normed_written, *table_written, table_clear, landed[E - 1])
        wait(pool, landed[E - 1])


_INS = ['x', 'ctx_768', 'g_xattn', 'g_ffn', 'L0_xattn_Wq', 'L0_xattn_bq', 'L0_xattn_Wk', 'L0_xattn_bk',
        'L0_xattn_Wv', 'L0_xattn_bv', 'L0_xattn_Wo', 'L0_xattn_bo', 'L0_ffn_router_w', 'L0_ffn_router_b',
        'L0_ffn_w1', 'L0_ffn_b1', 'L0_ffn_w2', 'L0_ffn_b2']
_OUTS = [((2, 2048, 512), 'float32')]


def kernel(**inputs):
    import numpy as _np
    import concourse.bacc as _bacc
    from concourse import mybir as _mybir
    from concourse.bass_utils import run_bass_kernel_spmd as _run

    nc = _bacc.Bacc("TRN2", target_bir_lowering=False, num_devices=1)
    arrays, args = {}, []
    for name in _INS:
        a = _np.ascontiguousarray(inputs[name])
        arrays[f"in_{name}_dram"] = a
        args.append(nc.dram_tensor(f"in_{name}_dram", a.shape, _mybir.dt.from_np(a.dtype), kind="ExternalInput").ap())
    for i, (shape, dtype) in enumerate(_OUTS):
        dt = _mybir.dt.from_np(_np.dtype(dtype))
        args.append(nc.dram_tensor(f"out_{i}_dram", shape, dt, kind="ExternalOutput").ap())
    moe_block_kernel(nc, *args)
    r = _run(nc, [arrays], core_ids=[0])
    got = tuple(r.results[0][f"out_{i}_dram"] for i in range(len(_OUTS)))
    return got[0]
```

```python
from contextlib import ExitStack

import concourse.bass as bass
from concourse import mybir

ALU = mybir.AluOpType
ACT = mybir.ActivationFunctionType
AX = mybir.AxisListType
F32 = mybir.dt.float32
F32R = mybir.dt.float32r
BF16 = mybir.dt.bfloat16
I32 = mybir.dt.int32
P = 128
BANK = 512


class Sem:

    def __init__(self, nc, ctx, name):
        self.sem = ctx.enter_context(nc.semaphore(name))
        self.value = 0

    def up(self, ins, by=1):
        ins.then_inc(self.sem, by)
        self.value += by
        return (self, self.value)

    def dma(self, ins):
        return self.up(ins, 16)


class Buf:

    def __init__(self, ap):
        self.ap = ap
        self.ready = ()
        self.free = ()


def moe_block_kernel(nc, x, ctx_in, g_xattn, g_ffn, Wq, bq, Wk, bk, Wv, bv, Wo, bo,
                     router_w, router_b, w1, b1, w2, b2, out):
    NB, SEQ, D = x.shape
    NKV, CK = ctx_in.shape[1:]
    E, _, FF = w1.shape
    H = 16
    DH = D // H
    TOK = NB * SEQ
    TOPK = 2
    CAP = -(-5 * TOK * TOPK // (4 * E))
    CLAMP = 10000.0
    SCALE = float(DH) ** -0.5
    EPS = 1e-5
    KD = D // P
    KC = CK // P
    NG = D // P
    HG = P // DH
    SUP = BANK
    TPS = SUP // P
    NS = TOK // SUP
    SPB = SEQ // SUP
    KEYS = H * NKV
    NCH = -(-KEYS // P)
    GK = HG * NKV
    HH = H // 2
    NF = FF // P
    ST = CAP // P
    HALF = CAP // 2
    CF = BANK // P
    NC = NF // CF
    NROW = E * ST
    FAR = 1.0e6
    assert CAP % P == 0 and HALF <= BANK and KEYS <= NCH * P and NROW <= P and GK <= BANK

    pairs = [[c for c in range(NCH) if c * P < (g + 1) * GK and (c + 1) * P > g * GK] for g in range(NG)]
    pair_at = {}
    for g in range(NG):
        for c in pairs[g]:
            pair_at[c, g] = len(pair_at)

    pe, act, dve, pool, sp = nc.tensor, nc.scalar, nc.vector, nc.gpsimd, nc.sync
    x_rows = x.rearrange("b s d -> (b s) d")
    out_rows = out.rearrange("b s d -> (b s) d")
    x_sup = x_rows.rearrange("(s t p) d -> s p t d", p=P, t=TPS)
    out_sup = out_rows.rearrange("(s t p) d -> s p t d", p=P, t=TPS)
    normed = nc.dram_tensor("normed_rows", (TOK, D), F32).ap()
    normed_sup = normed.rearrange("(s t p) d -> s p t d", p=P, t=TPS)

    top = ExitStack()
    with top:
        sems = {}

        def S(name):
            if name not in sems:
                sems[name] = Sem(nc, top, name)
            return sems[name]

        seen = {}

        def wait(eng, *events):
            for event in events:
                if event is None:
                    continue
                if isinstance(event, list) or (event and not isinstance(event[0], Sem)) or event == ():
                    wait(eng, *event)
                    continue
                sem, value = event
                if seen.get((id(eng), id(sem)), 0) < value:
                    seen[id(eng), id(sem)] = value
                    eng.wait_ge(sem.sem, value)

        def sb(ctx, name, shape, dt=F32):
            return ctx.enter_context(nc.sbuf_tensor(name, shape, dt))

        ring_a = [top.enter_context(nc.psum_tensor(f"ring_a{i}", [P, BANK], F32)) for i in range(2)]
        pair = [top.enter_context(nc.psum_tensor(f"pair{i}", [P, 2, BANK], F32)) for i in range(2)]
        ring_b = [top.enter_context(nc.psum_tensor(f"ring_b{i}", [P, BANK], F32)) for i in range(2)]
        bank_a = [Buf(t) for t in ring_a]
        bank_b = [Buf(t) for t in ring_b]
        score_pair = [Buf(t) for t in pair]
        turn = {"a": 0, "b": 0, "s": 0, "m": 0}

        def take(name, banks):
            turn[name] += 1
            return banks[(turn[name] - 1) % len(banks)]

        ident = sb(top, "ident", [P, P])
        ones_f = sb(top, "ones_f", [P, P])
        tanh_g = sb(top, "tanh_g", [P, 2])
        bias_cols = sb(top, "bias_cols", [P, 2 * KD])
        b1_cols = sb(top, "b1_cols", [P, E * NF])
        router_wT = sb(top, "router_wT", [P, KD, E])
        router_b_col = sb(top, "router_b_col", [E, 1])
        bo_rows = sb(top, "bo_rows", [P, D])
        mean_v = sb(top, "mean_v", [P, NG, NB])
        nan_sums = sb(top, "nan_sums", [P, 2 * TOK // P])
        nan_total = sb(top, "nan_total", [P, 1])
        no_nan = sb(top, "no_nan", [P, 1])
        keep_mask = sb(top, "keep_mask", [P, 1], I32)
        drop_mask = sb(top, "drop_mask", [P, 1], I32)
        mean_bits = sb(top, "mean_bits", [P, NG, NB], I32)
        stats = sb(top, "stats", [P, 2, TPS, 6])
        mean_var = sb(top, "mean_var", [P, TPS, 2])
        var_eps = sb(top, "var_eps", [P, TPS])
        half_bits = sb(top, "half_bits", [P, TPS], I32)
        rstd = sb(top, "rstd", [P, TPS])
        newton = sb(top, "newton", [P, TPS])
        NSM = 4
        smax = [sb(top, f"smax{i}", [P, HH]) for i in range(NSM)]
        ssum = [sb(top, f"ssum{i}", [P, HH]) for i in range(NSM)]
        slot_token = sb(top, "slot_token", [P, NROW], I32)
        slot_gate = sb(top, "slot_gate", [P, NROW])

        lay1 = ExitStack()
        Wq_hi = sb(lay1, "Wq_hi", [P, KD, D], F32R)
        Wq_lo = sb(lay1, "Wq_lo", [P, KD, D], F32R)
        k_block = sb(lay1, "k_block", [P, NB, NG, GK])
        v_pack = sb(lay1, "v_pack", [P, NB, len(pair_at), P])
        xT_hi = Buf(sb(lay1, "xT_hi", [P, KD, SUP], F32R))
        xT_lo = Buf(sb(lay1, "xT_lo", [P, KD, SUP], F32R))
        qT = [Buf(sb(lay1, f"qT{i}", [P, NG, SUP])) for i in range(2)]
        NP = 3
        probs = [Buf(sb(lay1, f"probs{i}", [P, NCH * P])) for i in range(NP)]
        pT = [Buf(sb(lay1, f"pT{i}", [P, NCH, 2 * P])) for i in range(2)]
        lay12 = ExitStack()
        raw = ExitStack()
        Wq_raw = sb(raw, "Wq_raw", [P, KD, D])
        Wo_raw = sb(raw, "Wo_raw", [P, KD, D])
        Wk_sb = sb(raw, "Wk_sb", [P, KC, D])
        Wv_sb = sb(raw, "Wv_sb", [P, KC, D])
        ctx_sb = sb(raw, "ctx_sb", [NKV, NB, CK])
        ctxT = sb(raw, "ctxT", [P, KC, NB * NKV])
        v_sb = sb(raw, "v_sb", [NKV, NB, D])
        inv_keys = sb(raw, "inv_keys", [P, 1])
        bias_rows = sb(raw, "bias_rows", [2 * KD, P])
        b1_rows = sb(raw, "b1_rows", [P, E * NF // P, P])
        bv_row = sb(raw, "bv_row", [1, D])
        bo_row = sb(raw, "bo_row", [1, D])
        rw_rows = sb(raw, "rw_rows", [E, D])
        gate_in = sb(raw, "gate_in", [P, 2])
        raw.close()
        attn_out = sb(lay12, "attn_out", [P, NG, TOK])
        xs = [Buf(sb(lay12, f"x_sup{i}", [P, TPS, D])) for i in range(2)]
        Wo_hi = sb(lay12, "Wo_hi", [P, KD, D], F32R)
        Wo_lo = sb(lay12, "Wo_lo", [P, KD, D], F32R)
        lay12.close()
        lay1.close()
        lay3 = top
        w_raw = [(Buf(sb(lay3, f"w1_raw{i}", [P, KD, BANK])), Buf(sb(lay3, f"w2_raw{i}", [P, CF, D])))
                 for i in range(2)]
        xg = Buf(sb(lay3, "gathered", [P, ST, D]))
        lay2 = ExitStack()
        NA = 4
        ao_hi = [Buf(sb(lay2, f"ao_hi{i}", [P, NG, P], F32R)) for i in range(NA)]
        ao_lo = [Buf(sb(lay2, f"ao_lo{i}", [P, NG, P], F32R)) for i in range(NA)]
        xn2 = [Buf(sb(lay2, f"xn2_{i}", [P, TPS, D])) for i in range(2)]
        xn2T = Buf(sb(lay2, "xn2T", [P, KD, SUP]))
        logitT = Buf(sb(lay2, "logitT", [E, SUP]))
        BT = 2 * TPS
        logits = sb(lay2, "logits", [P, BT, E])
        rest = sb(lay2, "rest", [P, BT, E])
        hit = sb(lay2, "hit", [P, BT, E])
        place = sb(lay2, "place", [P, BT, E])
        one_hot = sb(lay2, "one_hot", [P, TOPK, BT, E])
        chosen = sb(lay2, "chosen", [P, BT, E], BF16)
        taken = sb(lay2, "taken", [P, BT + 1, E], BF16)
        best = sb(lay2, "best", [P, TOPK, BT])
        best_no = sb(lay2, "best_no", [P, TOPK, BT])
        prior = sb(lay2, "prior", [P, TOPK, BT, E])
        pos = sb(lay2, "pos", [P, TOPK, BT])
        slot_hi = sb(lay2, "slot_hi", [P, TOPK, BT])
        slot_lo = sb(lay2, "slot_lo", [P, TOPK, BT])
        kept = sb(lay2, "kept", [P, TOPK, BT])
        away = sb(lay2, "away", [P, TOPK, BT])
        gap = sb(lay2, "gap", [P, BT])
        gexp = sb(lay2, "gexp", [P, BT])
        gden = sb(lay2, "gden", [P, BT])
        gate = sb(lay2, "gate", [P, TOPK, BT])
        at_lo = [Buf(sb(lay2, f"at_lo{i}", [P, P])) for i in range(4)]
        at_hi = [Buf(sb(lay2, f"at_hi{i}", [P, 2, NROW])) for i in range(4)]
        ones_b = sb(lay2, "ones_b", [P, P], BF16)
        before = sb(lay2, "before", [P, P], BF16)
        expert_no = sb(lay2, "expert_no", [P, E])
        expert_no_far = sb(lay2, "expert_no_far", [P, E])
        token_no = sb(lay2, "token_no", [P, TOK // P])
        row_no = sb(lay2, "row_no", [P, P])
        empty = sb(lay2, "empty", [P, NROW])
        lay2.close()
        w_split = [[Buf(sb(lay3, f"{n}_{h}{i}", [P, CF, BANK], F32R)) for n in ("w1", "w2") for h in ("hi", "lo")]
                   for i in range(2)]
        xgT = [(Buf(sb(lay3, f"xgT_hi{i}", [P, KD, CAP], F32R)), Buf(sb(lay3, f"xgT_lo{i}", [P, KD, CAP], F32R)))
               for i in range(2)]
        h_full = [Buf(sb(lay3, f"h_full{i}", [P, HALF])) for i in range(3)]
        NH = 4
        h_hi = [Buf(sb(lay3, f"h_hi{i}", [P, CAP], F32R)) for i in range(NH)]
        h_lo = [Buf(sb(lay3, f"h_lo{i}", [P, CAP], F32R)) for i in range(NH)]
        b2_rows = [Buf(sb(lay3, f"b2_rows{i}", [P, D])) for i in range(2)]
        y = Buf(sb(lay3, "y", [P, ST, D]))

        def row(v):
            return v.rearrange("(a n) -> a n", a=1)

        def bc(ap, shape, dim=None):
            return ap.to_broadcast(shape)

        def load_x(s):
            b = xs[s % NS % 2]
            wait(sp, b.free)
            b.ready = S(f"load_x{s % NS % 2}").dma(sp.dma_start(b.ap[:], x_sup[s % NS]))

        S_small = S("load_small")
        for dst, src in ((ctx_sb[:], ctx_in.rearrange("b j c -> j b c")),
                         (bias_rows[0:KD, :], bq.rearrange("(k p) -> k p", p=P)),
                         (bias_rows[KD:2 * KD, :], bk.rearrange("(k p) -> k p", p=P)),
                         (bv_row[:], row(bv)), (bo_row[:], row(bo)),
                         (rw_rows[:], router_w),
                         (router_b_col[:], router_b.rearrange("(e a) -> e a", a=1)),
                         (gate_in[:, 0:1], g_xattn.partition_broadcast(P)),
                         (gate_in[:, 1:2], g_ffn.partition_broadcast(P)),
                         (b1_rows[:], b1.rearrange("e (f p) -> (e f) p", p=P).rearrange("(r q) p -> q r p", q=P))):
            small = S_small.dma(act.dma_start(dst, src))
        wk_in = S("load_wk").dma(sp.dma_start(Wk_sb[:], Wk.rearrange("(k p) n -> p k n", p=P)))
        wv_in = S("load_wv").dma(sp.dma_start(Wv_sb[:], Wv.rearrange("(k p) n -> p k n", p=P)))
        load_x(0)
        wq_in = S("load_wq").dma(sp.dma_start(Wq_raw[:], Wq.rearrange("(k p) n -> p k n", p=P)))
        load_x(1)
        wo_in = S("load_wo").dma(sp.dma_start(Wo_raw[:], Wo.rearrange("(k p) n -> p k n", p=P)))

        const = S("pool_const")
        wait(pool, const.up(pool.memset(ident[:], 0.0)))
        const.up(pool.affine_select(out=ident[:], in_=ident[:], compare_op=ALU.not_equal, fill=1.0, base=0,
                                    pattern=[[-1, P]], channel_multiplier=1))
        const.up(pool.memset(inv_keys[:], 1.0 / NKV))
        ident_done = const.up(pool.memset(ones_f[:], 1.0))
        k_clear = const.up(pool.memset(k_block[:], 0.0))
        v_clear = const.up(pool.memset(v_pack[:], 0.0))
        for b in range(NP):
            const_done = const.up(pool.memset(probs[b].ap[:, KEYS:NCH * P], 0.0))

        def late_constants():
            wait(pool, attn_done)
            wait(pool, const.up(pool.memset(before[:], 1.0)))
            const.up(pool.affine_select(out=before[:], in_=before[:], compare_op=ALU.is_gt, fill=0.0, base=0,
                                        pattern=[[1, P]], channel_multiplier=-1))
            const.up(pool.memset(ones_b[:], 1.0))
            for dst, base, pattern, rows in ((expert_no, 0, [[1, E]], 0), (expert_no_far, 100, [[1, E]], 0),
                                             (row_no, 0, [[1, P]], 0), (token_no, 1, [[P, TOK // P]], 1)):
                done = const.up(pool.iota(dst[:], pattern=pattern, base=base, channel_multiplier=rows,
                                          allow_small_or_imprecise_dtypes=True))
            return done

        wait(act, small)
        tanh_done = S("act_tanh").up(act.activation(tanh_g[:], gate_in[:], ACT.Tanh))

        def evac_copy(eng, dst, src, sem):
            if eng is act:
                return sem.up(act.activation(dst, src, ACT.Copy))
            return sem.up(eng.tensor_copy(dst, src))

        wait(pe, small, ident_done)
        setup_pe, setup_dve = S("pe_setup"), S("dve_setup")
        for b in range(NB):
            bank = take("a", bank_a)
            wait(pe, bank.free)
            for k in range(KC):
                ins = pe.transpose(bank.ap[:, k * NKV:(k + 1) * NKV], ctx_sb[:, b, k * P:(k + 1) * P],
                                   ident[0:NKV, 0:NKV])
            wait(dve, setup_pe.up(ins))
            for k in range(KC):
                ctx_turned = setup_dve.up(dve.tensor_copy(ctxT[:, k, b * NKV:(b + 1) * NKV],
                                                          bank.ap[:, k * NKV:(k + 1) * NKV]))
            bank.free = ctx_turned
        bank = take("a", bank_a)
        wait(pe, bank.free)
        pe.transpose(bank.ap[:, 0:2 * KD], bias_rows[:], ident[0:2 * KD, 0:2 * KD])
        for k in range(KD):
            pe.transpose(bank.ap[:, 16 + k * E:16 + (k + 1) * E], rw_rows[:, k * P:(k + 1) * P], ident[0:E, 0:E])
        for r in range(E * NF // P):
            ins = pe.transpose(bank.ap[:, 128 + r * P:128 + (r + 1) * P], b1_rows[:, r, :], ident[:])
        wait(dve, setup_pe.up(ins))
        setup_dve.up(dve.tensor_copy(bias_cols[:], bank.ap[:, 0:2 * KD]))
        setup_dve.up(dve.tensor_copy(router_wT[:].rearrange("p k e -> p (k e)"), bank.ap[:, 16:16 + KD * E]))
        cols_done = setup_dve.up(dve.tensor_copy(b1_cols[:], bank.ap[:, 128:128 + E * NF]))
        bank.free = cols_done
        bank = take("a", bank_a)
        wait(pe, bank.free)
        wait(dve, setup_pe.up(pe.matmul(bank.ap[:], ones_f[0:1, :], bo_row[:], start=True, stop=True)), tanh_done)
        bank.free = setup_dve.up(dve.tensor_scalar(bo_rows[:], bank.ap[:], tanh_g[:, 0:1], None, ALU.mult))
        wait(pe, wk_in, ctx_turned)
        wait(dve, cols_done, k_clear)
        for g in range(NG):
            bank = take("a", bank_a)
            wait(pe, bank.free)
            for k in range(KC):
                ins = pe.matmul(bank.ap[:, 0:NB * NKV], Wk_sb[:, k, g * P:(g + 1) * P], ctxT[:, k, :],
                                start=k == 0, stop=k == KC - 1)
            wait(dve, setup_pe.up(ins))
            for b in range(NB):
                for a in range(HG):
                    q = slice(a * DH, (a + 1) * DH)
                    k_done = setup_dve.up(dve.tensor_scalar(
                        k_block[q, b, g, a * NKV:(a + 1) * NKV], bank.ap[q, b * NKV:(b + 1) * NKV],
                        bias_cols[q, KD + g:KD + g + 1], SCALE, ALU.add, ALU.mult))
            bank.free = k_done
        wait(pe, wv_in)
        pack = S("pack_v")
        for b in range(NB):
            bank = take("a", bank_a)
            wait(pe, bank.free)
            for k in range(KC):
                pe.matmul(bank.ap[0:NKV, :], ctxT[:, k, b * NKV:(b + 1) * NKV], Wv_sb[:, k, :], start=k == 0,
                          stop=False)
            ins = pe.matmul(bank.ap[0:NKV, :], ones_f[0:1, 0:NKV], bv_row[:], start=False, stop=True)
            wait(dve, setup_pe.up(ins))
            v_done = setup_dve.up(dve.tensor_copy(v_sb[:, b, :], bank.ap[0:NKV, :]))
            bank.free = v_done
        wait(sp, v_done, v_clear)
        for h in range(H):
            g = h // HG
            for c in pairs[g]:
                lo, hi = max(h * NKV, c * P), min((h + 1) * NKV, (c + 1) * P)
                if lo < hi:
                    packed = pack.dma(sp.dma_start(
                        v_pack[lo - c * P:hi - c * P, :, pair_at[c, g], (h % HG) * DH:(h % HG + 1) * DH],
                        v_sb[lo - h * NKV:hi - h * NKV, :, h * DH:(h + 1) * DH]))
        bank = take("a", bank_a)
        wait(pe, bank.free, v_done)
        for g in range(NG):
            for b in range(NB):
                ins = pe.matmul(bank.ap[:, g * NB + b:g * NB + b + 1], v_sb[:, b, g * P:(g + 1) * P],
                                inv_keys[0:NKV, :], start=True, stop=True)
        wait(dve, setup_pe.up(ins))
        mean_done = setup_dve.up(dve.tensor_copy(mean_v[:].rearrange("p g b -> p (g b)"), bank.ap[:, 0:NG * NB]))
        bank.free = mean_done
        wait(act, wq_in)
        wq_hi_done = S("act_wsplit").up(act.activation(Wq_hi[:], Wq_raw[:], ACT.Copy))
        wait(dve, wq_in, wq_hi_done)
        wq_done = setup_dve.up(dve.tensor_tensor(Wq_lo[:], Wq_raw[:], Wq_hi[:], ALU.subtract))

        def split_wo():
            wait(act, wo_in)
            hi = S("act_wsplit").up(act.activation(Wo_hi[:], Wo_raw[:], ACT.Copy))
            wait(pool, wo_in, hi)
            return S("pool_wo").up(pool.tensor_tensor(Wo_lo[:], Wo_raw[:], Wo_hi[:], ALU.subtract))

        def chained(sem, steps):
            for emit in steps:
                wait(dve, (sem, sem.value) if sem.value else None)
                sem.up(emit())
                yield

        chains = []

        def draw(n):
            for _ in range(n):
                if not chains:
                    return
                c = chains.pop(0)
                if next(c, chains) is not chains:
                    chains.append(c)

        def finish(c):
            for _ in c:
                pass
            if c in chains:
                chains.remove(c)

        ln = S("dve_ln")

        def stats_of(src, i, t):
            return ln.up(dve.bn_stats(stats[:, i, t, :], src[:, t, :]))

        def rstd_steps(i):
            def aggregate():
                for t in range(TPS - 1):
                    ln.up(dve.bn_aggr(mean_var[:, t, :], stats[:, i, t, :]))
                return dve.bn_aggr(mean_var[:, TPS - 1, :], stats[:, i, TPS - 1, :])
            yield aggregate
            yield lambda: dve.tensor_scalar(var_eps[:], mean_var[:, :, 1:2].rearrange("p t a -> p (t a)"), EPS, None,
                                            ALU.add)
            yield lambda: dve.tensor_scalar(half_bits[:], var_eps[:].bitcast(I32), 1, None, ALU.logical_shift_right)
            yield lambda: dve.tensor_scalar(rstd[:].bitcast(I32), half_bits[:], -1.0, float(0x5F3759DF), ALU.mult,
                                            ALU.add)
            for _ in range(3):
                yield lambda: dve.tensor_tensor(newton[:], rstd[:], rstd[:], ALU.mult)
                yield lambda: dve.tensor_tensor(newton[:], newton[:], var_eps[:], ALU.mult)
                yield lambda: dve.tensor_scalar(newton[:], newton[:], -0.5, 1.5, ALU.mult, ALU.add)
                yield lambda: dve.tensor_tensor(rstd[:], rstd[:], newton[:], ALU.mult)

        def normalise(dst, src):
            wait(dve, (ln, ln.value))
            for t in range(TPS):
                ln.up(dve.tensor_scalar(dst[:, t, :], src[:, t, :], mean_var[:, t, 0:1], rstd[:, t:t + 1],
                                        ALU.subtract, ALU.mult))
                yield

        def norm_x(s):
            b = xs[s % 2]
            wait(dve, b.ready)
            for t in range(TPS):
                stats_of(b.ap, s % 2, t)
                yield
            yield from chained(ln, rstd_steps(s % 2))
            yield from normalise(b.ap, b.ap)
            b.ready = (ln, ln.value)

        def turn_x(s, k):
            b = xs[s % 2]
            bank = take("a", bank_a)
            wait(pe, bank.free, b.ready)
            for t in range(TPS):
                ins = pe.transpose(bank.ap[:, t * P:(t + 1) * P], b.ap[:, t, k * P:(k + 1) * P], ident[:])
            turned = S("pe_turn_x").up(ins)
            wait(act, turned, xT_hi.free)
            hi = S("act_xT").up(act.activation(xT_hi.ap[:, k, :], bank.ap[:], ACT.Copy))
            wait(dve, turned, hi, xT_lo.free)
            lo = S("dve_xT").up(dve.tensor_tensor(xT_lo.ap[:, k, :], bank.ap[:], xT_hi.ap[:, k, :], ALU.subtract))
            bank.free = (hi, lo)
            xT_hi.ready, xT_lo.ready = hi, lo
            if k == KD - 1:
                b.free = turned

        def split_products(acc, ks, w_hi, w_lo, m_hi, m_lo, first=True, last=True):
            ins = None
            for i, k in enumerate(ks):
                for j, (w, m) in enumerate(((w_hi, m_lo), (w_lo, m_hi), (w_hi, m_hi))):
                    ins = pe.matmul(acc, w(k), m(k), start=first and i == 0 and j == 0,
                                    stop=last and i == len(ks) - 1 and j == 2)
            return ins

        def project_q(s, g):
            bank = take("a", bank_a)
            wait(pe, bank.free, xT_hi.ready, xT_lo.ready, wq_done)
            c = slice(g * P, (g + 1) * P)
            ins = split_products(bank.ap[:], range(KD), lambda k: Wq_hi[:, k, c], lambda k: Wq_lo[:, k, c],
                                 lambda k: xT_hi.ap[:, k, :], lambda k: xT_lo.ap[:, k, :])
            q_done = S("pe_q").up(ins)
            if g == NG - 1:
                xT_hi.free = xT_lo.free = q_done
            q = qT[s % 2]
            wait(act, q_done, q.free, cols_done)
            q.ready = bank.free = S("act_q").up(act.activation(q.ap[:, g, :], bank.ap[:], ACT.Identity,
                                                               bias=bias_cols[:, g:g + 1]))

        softmax = {}

        def scores(u):
            tile, half = divmod(u, 2)
            s, t = divmod(tile, TPS)
            b = s // SPB
            pr = probs[tile % NP]
            sc = take("s", score_pair)
            wait(pe, sc.free, qT[s % 2].ready, k_done)
            for j in range(2):
                ins = pe.matmul(sc.ap[:, j, 0:GK], qT[s % 2].ap[:, 2 * half + j, t * P:(t + 1) * P],
                                k_block[:, b, 2 * half + j, :], start=True, stop=True)
            scored = S("pe_scores").up(ins)
            if u % (2 * TPS) == 2 * TPS - 1:
                qT[s % 2].free = scored
            sc3 = sc.ap[:, :, 0:GK].rearrange("p j (a n) -> p j a n", n=NKV)
            i = u % NSM
            n = S("dve_softmax")
            d = pr.ap[:, half * HH * NKV:(half + 1) * HH * NKV]
            wait(act, scored, pr.free)
            nan_seen = S("act_nan").up(act.activation(d.rearrange("p (j n) -> p j n", j=2), sc.ap[:, :, 0:GK],
                                                      ACT.Tanh, accum_out=nan_sums[:, u:u + 1]))
            mx = smax[i]
            draw(1)
            wait(dve, nan_seen)
            clipped = n.up(dve.tensor_scalar(d.rearrange("p (j a n) -> p j a n", j=2, n=NKV), sc3, -CLAMP, CLAMP,
                                             ALU.max, ALU.min))
            draw(2)
            wait(dve, clipped, softmax.get(u - NSM, {}).get("all"))
            d3 = d.rearrange("p (a n) -> p a n", n=NKV)
            greatest = n.up(dve.tensor_reduce(mx[:], d3, AX.X, ALU.max))
            sc.free = clipped
            wait(pool, greatest)
            mxb = mx[:].rearrange("p (a o) -> p a o", o=1).to_broadcast([P, HH, NKV])
            softmax[u] = {"less": S("pool_less").up(pool.tensor_tensor(d3, d3, mxb, ALU.subtract))}

        def normal_probs(u):
            tile, half = divmod(u, 2)
            pr = probs[tile % NP]
            d = pr.ap[:, half * HH * NKV:(half + 1) * HH * NKV]
            d3 = d.rearrange("p (a n) -> p a n", n=NKV)
            sm = ssum[u % NSM]
            wait(act, softmax[u]["less"])
            draw(1)
            e = S("act_exp").up(act.activation(d, d, ACT.Exp))
            wait(dve, e)
            n = S("dve_softmax")
            total = n.up(dve.tensor_reduce(sm[:], d3, AX.X, ALU.add))
            draw(1)
            wait(dve, total)
            r = n.up(dve.reciprocal(sm[:], sm[:]))
            wait(pool, r, e)
            smb = sm[:].rearrange("p (a o) -> p a o", o=1).to_broadcast([P, HH, NKV])
            pr.ready = S("pool_probs").up(pool.tensor_tensor(d3, d3, smb, ALU.mult))
            softmax[u]["all"] = (pr.ready, r)

        def turn_probs(tile, part):
            pr, dst = probs[tile % NP], pT[tile // 2 % 2]
            t = tile % 2
            for c0 in (range(0, 8, 4) if part == 0 else range(8, NCH, 4)):
                cs = range(c0, min(c0 + 4, NCH))
                bank = take("b", bank_b)
                wait(pe, bank.free, pr.ready, const_done)
                for c in cs:
                    ins = pe.transpose(bank.ap[:, (c - c0) * P:(c - c0 + 1) * P], pr.ap[:, c * P:(c + 1) * P], ident[:])
                turned = S("pe_turn_p").up(ins)
                eng = dve if c0 == 4 else act
                wait(eng, turned, dst.free)
                bank.free = evac_copy(eng, dst.ap[:, cs[0]:cs[-1] + 1, t * P:(t + 1) * P],
                                      bank.ap[:, 0:len(cs) * P].rearrange("p (c n) -> p c n", n=P),
                                      S("act_pT" if eng is act else "dve_pT"))
                dst.ready = (*dst.ready, bank.free)
            pr.free = turned

        def attend(two, g):
            b = two * 2 // (TPS * SPB)
            src = pT[two % 2]
            bank = take("a", bank_a)
            wait(pe, bank.free, src.ready, packed)
            for c in pairs[g]:
                ins = pe.matmul(bank.ap[:, 0:2 * P], v_pack[:, b, pair_at[c, g], :], src.ap[:, c, :],
                                start=c == pairs[g][0], stop=c == pairs[g][-1])
            done = S("pe_attend").up(ins)
            wait(act, done, raw_free)
            bank.free = S("act_attn").up(act.activation(attn_out[:, g, two * 2 * P:(two + 1) * 2 * P],
                                                        bank.ap[:, 0:2 * P], ACT.Copy))
            if g == NG - 1:
                src.ready = ()
                src.free = done
            return bank.free

        finish(norm_x(0))
        wo_done = split_wo()
        raw_free = (wq_done, wo_done, packed, mean_done)
        for k in range(KD):
            turn_x(0, k)
        for g in range(NG):
            project_q(0, g)
        load_x(2)
        finish(norm_x(1))
        for k in range(KD):
            turn_x(1, k)
        load_x(3)
        UNITS = 2 * TPS
        units = UNITS * NS
        TURN, ATTEND = 5, 9
        for u in range(units + ATTEND + 1):
            s, part = divmod(u, UNITS)
            turning = part == UNITS - 1 and s + 2 < NS
            if part == 0 and s + 2 < NS:
                norming = norm_x(s + 2)
                chains.append(norming)
            if turning:
                finish(norming)
                for k in range(KD // 2):
                    turn_x(s + 2, k)
            if u < units:
                scores(u)
            if 1 <= u <= units:
                normal_probs(u - 1)
            if turning:
                for k in range(KD // 2, KD):
                    turn_x(s + 2, k)
                load_x(s + 4)
            if s + 1 < NS and part % 2 == 0:
                project_q(s + 1, part // 2)
            if 0 <= u - ATTEND < units:
                attn_done = attend((u - ATTEND) // 4, (u - ATTEND) % 4)
            if 0 <= u - TURN < units:
                turn_probs(*divmod(u - TURN, 2))
            draw(2)

        guard = S("dve_guard")
        wait(dve, (S("act_nan"), S("act_nan").value))
        wait(pe, guard.up(dve.tensor_reduce(nan_total[:], nan_sums[:], AX.X, ALU.add)))
        bank = take("a", bank_a)
        wait(pe, bank.free)
        summed = S("pe_guard").up(pe.matmul(bank.ap[:, 0:1], ones_f[:], nan_total[:], start=True, stop=True))
        wait(dve, summed)
        wait(dve, guard.up(dve.tensor_copy(nan_total[:], bank.ap[:, 0:1])))
        bank.free = (guard, guard.value)
        wait(dve, guard.up(dve.tensor_tensor(no_nan[:], nan_total[:], nan_total[:], ALU.is_equal)))
        guard.up(dve.tensor_scalar(drop_mask[:], no_nan[:], 1.0, None, ALU.subtract))
        wait(dve, guard.up(dve.tensor_scalar(keep_mask[:], no_nan[:], -1.0, None, ALU.mult)))
        wait(dve, guard.up(dve.tensor_tensor(mean_bits[:].rearrange("p g b -> p (g b)"),
                                             mean_v[:].bitcast(I32).rearrange("p g b -> p (g b)"),
                                             drop_mask[:].to_broadcast([P, NG * NB]), ALU.bitwise_and)))

        constants_done = late_constants()
        route = S("dve_route")
        stored = S("store_out")
        stored_norm = [S("store_normed0"), S("store_normed1")]
        wait(dve, attn_done)
        route.up(dve.memset(taken[:, 0, :], 0.0))
        table_bank = Buf(pair[1][:, 1, :])
        table_bank.free = (score_pair[0].free, score_pair[1].free)
        logit_bank, logit_turn_bank, count_bank = (Buf(pair[0][:, 0, :]), Buf(pair[0][:, 1, :]), Buf(pair[1][:, 0, :]))
        for b in (logit_bank, logit_turn_bank, count_bank):
            b.free = table_bank.free
        NT = TOK // P
        guarded = {}

        def guard_tile(s, g):
            bits = attn_out[:, g, s * SUP:(s + 1) * SUP].bitcast(I32)
            guarded[s] = guard.up(dve.tensor_scalar(bits, bits, keep_mask[:, 0:1],
                                                    mean_bits[:, g, s // SPB:s // SPB + 1],
                                                    ALU.bitwise_and, ALU.bitwise_or))

        def split_attn(v):
            hi, lo = ao_hi[v % NA], ao_lo[v % NA]
            src = attn_out[:, :, v * P:(v + 1) * P]
            wait(act, guarded[v // TPS], hi.free)
            hi.ready = S("act_ao").up(act.activation(hi.ap[:], src, ACT.Copy))
            wait(pool, hi.ready, lo.free)
            lo.ready = S("pool_ao").up(pool.tensor_tensor(lo.ap[:], src, hi.ap[:], ALU.subtract))

        based = {}

        def add_bo(v):
            s, t = divmod(v, TPS)
            b = xs[s % 2]
            wait(pool, b.ready)
            based[v] = S("pool_base").up(pool.tensor_tensor(b.ap[:, t, :], b.ap[:, t, :], bo_rows[:], ALU.add))

        def project_out(v):
            bank = take("a", bank_a)
            hi, lo = ao_hi[v % NA], ao_lo[v % NA]
            wait(pe, bank.free, hi.ready, lo.ready, wo_done)
            ins = split_products(bank.ap[:], range(KD), lambda k: hi.ap[:, k, :], lambda k: lo.ap[:, k, :],
                                 lambda k: Wo_hi[:, k, :], lambda k: Wo_lo[:, k, :])
            hi.free = lo.free = S("pe_y").up(ins)
            return bank

        def residual(v, bank):
            s, t = divmod(v, TPS)
            b = xs[s % 2]
            wait(dve, (S("pe_y"), S("pe_y").value), based[v])
            added = S("dve_resid").up(dve.scalar_tensor_tensor(
                out=b.ap[:, t, :], in0=bank.ap[:], scalar=tanh_g[:, 0:1], in1=b.ap[:, t, :], op0=ALU.mult,
                op1=ALU.add))
            bank.free = added
            draw(2)
            wait(dve, added)
            stats_of(b.ap, s % 2, t)
            if t == TPS - 1:
                wait(sp, added)
                b.free = (stored.dma(sp.dma_start(out_sup[s], b.ap[:])),)

        def norm_rows(s):
            b, n = xs[s % 2], xn2[s % 2]
            yield from chained(ln, rstd_steps(s % 2))
            wait(dve, n.free)
            yield from normalise(n.ap, b.ap)
            n.ready = (ln, ln.value)
            b.free = (*b.free, n.ready)
            wait(sp, n.ready)
            n.free = (stored_norm[s % 2].dma(sp.dma_start(normed_sup[s], n.ap[:])),)

        def turn_rows_out(s, k):
            n = xn2[s % 2]
            bank = take("b", bank_b)
            wait(pe, bank.free, n.ready)
            for t in range(TPS):
                ins = pe.transpose(bank.ap[:, t * P:(t + 1) * P], n.ap[:, t, k * P:(k + 1) * P], ident[:])
            turned = S("pe_turn_n").up(ins)
            wait(act, turned, xn2T.free)
            xn2T.ready = bank.free = S("act_nT").up(act.activation(xn2T.ap[:, k, :], bank.ap[:], ACT.Copy))
            if k == KD - 1:
                n.free = (*n.free, turned)

        def router(s):
            wait(pe, logit_bank.free, xn2T.ready)
            for k in range(KD):
                ins = pe.matmul(logit_bank.ap[0:E, :], router_wT[:, k, :], xn2T.ap[:, k, :], start=k == 0,
                                stop=k == KD - 1)
            xn2T.free = S("pe_router").up(ins)
            wait(act, xn2T.free, logitT.free)
            logitT.ready = logit_bank.free = S("act_logit").up(act.activation(
                logitT.ap[:], logit_bank.ap[0:E, :], ACT.Identity, bias=router_b_col[:]))

        def turn_logits(s, at):
            wait(pe, logitT.ready, logit_turn_bank.free)
            for t in range(TPS):
                ins = pe.transpose(logit_turn_bank.ap[:, t * E:(t + 1) * E], logitT.ap[:, t * P:(t + 1) * P],
                                   ident[0:E, 0:E])
            logitT.free = S("pe_router").up(ins)
            wait(dve, logitT.free, (route, route.value))
            logit_turn_bank.free = route.up(dve.tensor_copy(
                logits[:, at:at + TPS, :].rearrange("p t e -> p (t e)"), logit_turn_bank.ap[:, 0:TPS * E]))

        table_products = [0]

        def route_batch(v0, nt):
            def over_e(ap):
                return ap.rearrange("p (t o) -> p t o", o=1).to_broadcast([P, nt, E])

            def over_t(ap):
                return ap.rearrange("p (o e) -> p o e", o=1).to_broadcast([P, nt, E])

            T = slice(0, nt)
            oh = [one_hot[:, k, T, :] for k in range(TOPK)]

            def choose():
                for k, src in enumerate((logits[:, T, :], rest[:, T, :])):
                    yield lambda: dve.tensor_reduce(best[:, k, T], src, AX.X, ALU.max)
                    yield lambda: dve.tensor_tensor(hit[:, T, :], src, over_e(best[:, k, T]), ALU.is_equal)
                    yield lambda: dve.scalar_tensor_tensor(out=place[:, T, :], in0=hit[:, T, :], scalar=-100.0,
                                                           in1=over_t(expert_no_far[:]), op0=ALU.mult, op1=ALU.add)
                    yield lambda: dve.tensor_reduce(best_no[:, k, T], place[:, T, :], AX.X, ALU.min)
                    yield lambda: dve.tensor_tensor(oh[k], over_t(expert_no[:]), over_e(best_no[:, k, T]),
                                                    ALU.is_equal)
                    if k == 0:
                        yield lambda: dve.scalar_tensor_tensor(out=rest[:, T, :], in0=oh[0], scalar=-3.0e38,
                                                               in1=logits[:, T, :], op0=ALU.mult, op1=ALU.add)
                yield lambda: dve.tensor_tensor(chosen[:, T, :], oh[0], oh[1], ALU.add)
                for t in range(nt):
                    yield lambda: dve.tensor_tensor(taken[:, t + 1, :], taken[:, t, :], chosen[:, t, :], ALU.add)
                yield lambda: dve.tensor_tensor(gap[:, T], best[:, 1, T], best[:, 0, T], ALU.subtract)

            wait(dve, constants_done)
            yield from chained(route, choose())
            chosen_all = (route, route.value)
            wait(pe, chosen_all, count_bank.free)
            acc = count_bank.ap[:, 0:nt * E]
            pe.matmul(acc, before[:], chosen[:, T, :].rearrange("p t e -> p (t e)"), start=True, stop=False)
            counted = S("pe_count").up(pe.matmul(acc, ones_b[:], taken[:, T, :].rearrange("p t e -> p (t e)"),
                                                 start=False, stop=True))
            wait(act, chosen_all)
            odds = S("act_gate").up(act.activation(gexp[:, T], gap[:, T], ACT.Exp))
            yield

            def place_them():
                for k in range(TOPK):
                    yield lambda: dve.tensor_tensor(
                        prior[:, k, T, :], count_bank.ap[:, 0:nt * E].rearrange("p (t e) -> p t e", e=E), oh[k],
                        ALU.mult)
                yield lambda: dve.tensor_reduce(pos[:, :, T], prior[:, :, T, :], AX.X, ALU.add)
                yield lambda: dve.tensor_scalar(kept[:, :, T], pos[:, :, T], float(CAP), None, ALU.is_lt)
                yield lambda: dve.tensor_scalar(away[:, :, T], kept[:, :, T], -FAR, FAR, ALU.mult, ALU.add)
                yield lambda: dve.tensor_scalar(slot_hi[:, :, T], pos[:, :, T], float(P), None, ALU.is_ge)
                for m in range(2, ST):
                    yield lambda: dve.scalar_tensor_tensor(out=slot_hi[:, :, T], in0=pos[:, :, T],
                                                           scalar=float(m * P), in1=slot_hi[:, :, T], op0=ALU.is_ge,
                                                           op1=ALU.add)
                yield lambda: dve.scalar_tensor_tensor(out=slot_lo[:, :, T], in0=slot_hi[:, :, T], scalar=-float(P),
                                                       in1=pos[:, :, T], op0=ALU.mult, op1=ALU.add)
                yield lambda: dve.scalar_tensor_tensor(out=slot_hi[:, :, T], in0=best_no[:, :, T], scalar=float(ST),
                                                       in1=slot_hi[:, :, T], op0=ALU.mult, op1=ALU.add)
                yield lambda: dve.tensor_tensor(slot_hi[:, :, T], slot_hi[:, :, T], away[:, :, T], ALU.add)
                yield lambda: dve.tensor_scalar(gden[:, T], gexp[:, T], 1.0, None, ALU.add)
                yield lambda: dve.reciprocal(gate[:, 0, T], gden[:, T])
                yield lambda: dve.tensor_tensor(gate[:, 1, T], gexp[:, T], gate[:, 0, T], ALU.mult)
                yield lambda: dve.tensor_tensor(gate[:, :, T], gate[:, :, T], kept[:, :, T], ALU.mult)
                yield lambda: dve.tensor_tensor(gden[:, T], gate[:, 0, T], gate[:, 1, T], ALU.add)
                yield lambda: dve.tensor_scalar(gden[:, T], gden[:, T], 1e-9, None, ALU.add)
                yield lambda: dve.reciprocal(gden[:, T], gden[:, T])
                yield lambda: dve.tensor_scalar(gden[:, T], gden[:, T], tanh_g[:, 1:2], None, ALU.mult)
                yield lambda: dve.tensor_tensor(gate[:, :, T], gate[:, :, T],
                                                gden[:, T].rearrange("p (o t) -> p o t", o=1)
                                                .to_broadcast([P, TOPK, nt]), ALU.mult)

            carry = lambda: dve.tensor_copy(taken[:, 0, :], taken[:, nt, :])
            wait(dve, counted, odds)
            yield from chained(route, place_them())
            count_bank.free = (route, route.value)
            yield from chained(route, [carry])
            one = S("dve_one_hot")
            wait(dve, (route, route.value))
            for t in range(nt):
                for k in range(TOPK):
                    i = table_products[0] % len(at_lo)
                    lo, hi = at_lo[i], at_hi[i]
                    col = slot_hi[:, k, t:t + 1]
                    wait(dve, lo.free)
                    one.up(dve.tensor_scalar(lo.ap[:], row_no[:], slot_lo[:, k, t:t + 1], None, ALU.is_equal))
                    yield
                    one.up(dve.tensor_scalar(hi.ap[:, 0, :], row_no[:, 0:NROW], col, token_no[:, v0 + t:v0 + t + 1],
                                             ALU.is_equal, ALU.mult))
                    yield
                    made = one.up(dve.tensor_scalar(hi.ap[:, 1, :], row_no[:, 0:NROW], col, gate[:, k, t:t + 1],
                                                    ALU.is_equal, ALU.mult))
                    wait(pe, made, table_bank.free)
                    table_products[0] += 1
                    lo.free = S("pe_table").up(pe.matmul(
                        table_bank.ap[:, 0:2 * NROW], lo.ap[:], hi.ap[:].rearrange("p c r -> p (c r)"),
                        start=table_products[0] == 1, stop=table_products[0] == TOPK * NT))
                    yield

        def load_chunk(n):
            e, c = divmod(n, NC)
            for i, (buf, src) in enumerate(zip(w_raw[n % 2], (
                    w1[e].rearrange("(k p) f -> p k f", p=P)[:, :, c * BANK:(c + 1) * BANK],
                    w2[e].rearrange("(f p) d -> p f d", p=P)[:, c * CF:(c + 1) * CF, :]))):
                wait(sp, buf.free)
                buf.ready = S(f"load_w{i + 1}_{n % 2}").dma(sp.dma_start(buf.ap[:], src))

        def split_chunk(n, i):
            src, hi, lo = w_raw[n % 2][i], w_split[n % 2][2 * i], w_split[n % 2][2 * i + 1]
            wait(act, src.ready, hi.free, stage2_done)
            hi.ready = S("act_whi").up(act.activation(hi.ap[:], src.ap[:], ACT.Copy))
            wait(dve, src.ready, hi.ready, lo.free, stage2_done)
            lo.ready = S("dve_wlo").up(dve.tensor_tensor(lo.ap[:], src.ap[:], hi.ap[:], ALU.subtract))
            src.free = (hi.ready, lo.ready)

        for b in (*ao_hi, *ao_lo, *xn2, xn2T, logitT, *at_lo, *at_hi):
            b.free = (attn_done, b.free)
        for b in (*w_raw[0], *w_raw[1]):
            b.free = attn_done
        batches = []
        left = NS
        while left:
            n = 2 if left > 2 else 1
            batches.append((NS - left, n))
            left -= n
        batch_of = {s: (s0, n) for s0, n in batches for s in range(s0, s0 + n)}
        tasks = {}

        def at_unit(v, f, *args):
            tasks.setdefault(v, []).append((f, args))

        def start_chain(c):
            chains.insert(0, c)
            return c

        routing = [None]

        def start_routing(s0, n):
            routing[0] = start_chain(route_batch(s0 * TPS, n * TPS))

        def end_routing():
            if routing[0]:
                finish(routing[0])

        norming = {}

        def start_norm(s):
            norming[s] = start_chain(norm_rows(s))

        def end_norm(s):
            finish(norming[s])
            if s + 2 < NS:
                load_x(s + 2)

        for s in range(NS):
            v = (s + 1) * TPS
            s0, n = batch_of[s]
            normed_at, turned_at, router_at, routed_at = ((0, 0, 0, 0) if s == NS - 1 else
                                                             (1, 1, 2, 3) if s == NS - 2 else (1, 2, 3, 4))
            at_unit(v, start_norm, s)
            at_unit(v + normed_at, end_norm, s)
            for k in range(KD):
                at_unit(v + (normed_at if k < KD // 2 else turned_at), turn_rows_out, s, k)
            at_unit(v + router_at, router, s)
            v += routed_at
            if s == s0:
                at_unit(v, end_routing)
            at_unit(v, turn_logits, s, (s - s0) * TPS)
            if s == s0 + n - 1:
                at_unit(v, start_routing, s0, n)
        at_unit(NT - 2 * TPS, load_chunk, 0)
        at_unit(NT - 2 * TPS, load_chunk, 1)
        for g in range(NG):
            guard_tile(0, g)
        split_attn(0)
        split_attn(1)
        add_bo(0)
        add_bo(1)
        for v in range(NT + 1):
            if v < NT:
                bank = project_out(v)
            draw(4)
            for f, args in tasks.get(v, ()):
                f(*args)
                draw(2)
            if v < NT:
                s, t = divmod(v, TPS)
                residual(v, bank)
                draw(4)
                if s + 1 < NS and t < 2:
                    guard_tile(s + 1, 2 * t)
                    draw(2)
                    guard_tile(s + 1, 2 * t + 1)
                if v + 2 < NT:
                    split_attn(v + 2)
                    add_bo(v + 2)
                draw(5)
        assert not [v for v in tasks if v > NT]
        end_routing()

        out_written = (stored, stored.value)
        normed_written = tuple((q, q.value) for q in stored_norm)
        wait(dve, (S("pe_table"), S("pe_table").value))
        route.up(dve.tensor_copy(slot_gate[:], table_bank.ap[:, NROW:2 * NROW]))
        wait(dve, route.up(dve.tensor_scalar(empty[:], table_bank.ap[:, 0:NROW], 1.0, FAR, ALU.is_lt, ALU.mult)))
        table_done = route.up(dve.scalar_tensor_tensor(out=slot_token[:], in0=table_bank.ap[:, 0:NROW], scalar=-1.0,
                                                       in1=empty[:], op0=ALU.add, op1=ALU.add))
        stage2_done = (table_done, out_written, *normed_written)

        all_banks = [Buf(ring_a[0]), Buf(ring_a[1]), Buf(pair[0][:, 0, :]), Buf(pair[0][:, 1, :]),
                     Buf(pair[1][:, 0, :]), Buf(pair[1][:, 1, :]), Buf(ring_b[0]), Buf(ring_b[1])]
        for n, old in enumerate((bank_a[0], bank_a[1], logit_bank, logit_turn_bank, count_bank, table_bank,
                                 bank_b[0], bank_b[1])):
            all_banks[n].free = table_done if old is table_bank else old.free
        y_banks, m_banks = all_banks[:ST], all_banks[ST:]

        wait(pool, attn_done)
        cleared = S("pool_clear").up(pool.memset(xg.ap[:], 0.0))
        wait(pool, cleared)

        def gather(e):
            wait(pool, table_done, *normed_written, xg.free)
            for t in range(ST):
                i = e * ST + t
                xg.ready = S("gather").dma(pool.indirect_dma_start(
                    xg.ap[:, t, :], None, normed, bass.IndirectOffsetOnAxis(ap=slot_token[:, i:i + 1], axis=0),
                    bounds_check=TOK - 1, oob_is_err=False))

        def load_b2(e):
            b = b2_rows[e % 2]
            wait(sp, b.free, stage2_done)
            b.ready = S(f"load_b2_{e % 2}").dma(sp.dma_start(b.ap[:], b2[e].partition_broadcast(P)))

        def turn_rows(e, t):
            hi_b, lo_b = xgT[e % 2]
            bank = take("m", m_banks)
            wait(pe, bank.free, xg.ready)
            for k in range(KD):
                ins = pe.transpose(bank.ap[:, k * P:(k + 1) * P], xg.ap[:, t, k * P:(k + 1) * P], ident[:])
            turned = S("pe_turn_g").up(ins)
            sl = slice(t * P, (t + 1) * P)
            src = bank.ap[:, :].rearrange("p (k n) -> p k n", n=P)
            wait(act, turned, hi_b.free, stage2_done)
            hi = S("act_gT").up(act.activation(hi_b.ap[:, :, sl], src, ACT.Copy))
            wait(dve, turned, hi, lo_b.free, stage2_done)
            lo = S("dve_gT").up(dve.tensor_tensor(lo_b.ap[:, :, sl], src, hi_b.ap[:, :, sl], ALU.subtract))
            bank.free = (hi, lo)
            hi_b.ready, lo_b.ready = hi, lo
            if t == ST - 1:
                xg.free = turned

        def hidden(q, half):
            e, f = divmod(q, NF)
            n, j = divmod(q, CF)
            w_hi, w_lo = w_split[n % 2][0], w_split[n % 2][1]
            x_hi, x_lo = xgT[e % 2]
            bank = take("m", m_banks)
            wait(pe, bank.free, x_hi.ready, x_lo.ready, w_hi.ready, w_lo.ready)
            sl = slice(half * HALF, (half + 1) * HALF)
            c = slice(j * P, (j + 1) * P)
            ins = split_products(bank.ap[:, 0:HALF], range(KD), lambda k: w_hi.ap[:, k, c], lambda k: w_lo.ap[:, k, c],
                                 lambda k: x_hi.ap[:, k, sl], lambda k: x_lo.ap[:, k, sl])
            done = S("pe_hidden").up(ins)
            if half == 1:
                if j == CF - 1:
                    w_hi.free = w_lo.free = done
                if f == NF - 1:
                    x_hi.free = x_lo.free = done
            hh, hl, hf = h_hi[q % NH], h_lo[q % NH], h_full[(2 * q + half) % len(h_full)]
            bias = b1_cols[:, q:q + 1]
            wait(act, done, hf.free, stage2_done)
            full = S("act_gelu").up(act.activation(hf.ap[:], bank.ap[:, 0:HALF], ACT.Gelu, bias=bias))
            wait(act, hh.free)
            hi = S("act_gelu").up(act.activation(hh.ap[:, sl], bank.ap[:, 0:HALF], ACT.Gelu, bias=bias))
            bank.free = hi
            wait(dve, full, hi, hl.free, stage2_done)
            lo = S("dve_hlo").up(dve.tensor_tensor(hl.ap[:, sl], hf.ap[:], hh.ap[:, sl], ALU.subtract))
            hf.free = lo
            hh.ready, hl.ready = hi, lo

        def start_y(e):
            b = b2_rows[e % 2]
            wait(dve, b.ready, y.free, stage2_done)
            for t in range(ST):
                i = e * ST + t
                y.ready = S("dve_y").up(dve.tensor_scalar(y.ap[:, t, :], b.ap[:], slot_gate[:, i:i + 1], None, ALU.mult))
            b.free = y.ready

        def down(q):
            e, f = divmod(q, NF)
            n, j = divmod(q, CF)
            w_hi, w_lo = w_split[n % 2][2], w_split[n % 2][3]
            hh, hl = h_hi[q % NH], h_lo[q % NH]
            for t in range(ST):
                bank = y_banks[t]
                sl = slice(t * P, (t + 1) * P)
                wait(pe, hh.ready, hl.ready, w_hi.ready, w_lo.ready, bank.free if f == 0 else None)
                ins = split_products(bank.ap[:, :], [j], lambda k: hh.ap[:, sl], lambda k: hl.ap[:, sl],
                                     lambda k: w_hi.ap[:, k, :], lambda k: w_lo.ap[:, k, :],
                                     first=f == 0, last=f == NF - 1)
                if f == NF - 1:
                    finish_y(e, t, bank, S("pe_down").up(ins))
            done = S("pe_down").up(ins) if f < NF - 1 else (S("pe_down"), S("pe_down").value)
            hh.free = hl.free = done
            if j == CF - 1:
                w_hi.free = w_lo.free = done

        def finish_y(e, t, bank, product):
            i = e * ST + t
            wait(dve, product, y.ready)
            bank.free = S("dve_yout").up(dve.scalar_tensor_tensor(
                out=y.ap[:, t, :], in0=bank.ap[:, :], scalar=slot_gate[:, i:i + 1], in1=y.ap[:, t, :], op0=ALU.mult,
                op1=ALU.add))
            wait(pool, bank.free, out_written, landed[e - 1] if e else None)
            landed[e] = S("scatter_out").dma(pool.indirect_dma_start(
                out_rows, bass.IndirectOffsetOnAxis(ap=slot_token[:, i:i + 1], axis=0), y.ap[:, t, :], None,
                bounds_check=TOK - 1, oob_is_err=False, compute_op=ALU.add))
            y.free = landed[e]

        landed = {}
        LAG = 2
        gather(0)
        load_b2(0)
        split_chunk(0, 0)
        for t in range(ST):
            turn_rows(0, t)
        split_chunk(0, 1)
        total = E * NF
        for q in range(total + LAG):
            if q < total:
                e, f = divmod(q, NF)
                n, j = divmod(q, CF)
                if e + 1 < E:
                    if f == 2:
                        gather(e + 1)
                        load_b2(e + 1)
                    if 8 <= f < 8 + ST:
                        turn_rows(e + 1, f - 8)
                if f == 5:
                    start_y(e)
                hidden(q, 0)
                hidden(q, 1)
                if n + 1 < E * NC:
                    if j == CF - 2:
                        split_chunk(n + 1, 0)
                    if j == CF - 1:
                        split_chunk(n + 1, 1)
                        if n + 3 < E * NC + 1:
                            load_chunk(n + 2) if n + 2 < E * NC else None
            if q >= LAG:
                down(q - LAG)
        wait(sp, out_written, *normed_written, landed[E - 1])
        wait(pool, landed[E - 1])


_INS = ['x', 'ctx_768', 'g_xattn', 'g_ffn', 'L0_xattn_Wq', 'L0_xattn_bq', 'L0_xattn_Wk', 'L0_xattn_bk',
        'L0_xattn_Wv', 'L0_xattn_bv', 'L0_xattn_Wo', 'L0_xattn_bo', 'L0_ffn_router_w', 'L0_ffn_router_b',
        'L0_ffn_w1', 'L0_ffn_b1', 'L0_ffn_w2', 'L0_ffn_b2']
_OUTS = [((2, 2048, 512), 'float32')]


def kernel(**inputs):
    import numpy as _np
    import concourse.bacc as _bacc
    from concourse import mybir as _mybir
    from concourse.bass_utils import run_bass_kernel_spmd as _run

    nc = _bacc.Bacc("TRN2", target_bir_lowering=False, num_devices=1)
    arrays, args = {}, []
    for name in _INS:
        a = _np.ascontiguousarray(inputs[name])
        arrays[f"in_{name}_dram"] = a
        args.append(nc.dram_tensor(f"in_{name}_dram", a.shape, _mybir.dt.from_np(a.dtype), kind="ExternalInput").ap())
    for i, (shape, dtype) in enumerate(_OUTS):
        dt = _mybir.dt.from_np(_np.dtype(dtype))
        args.append(nc.dram_tensor(f"out_{i}_dram", shape, dt, kind="ExternalOutput").ap())
    moe_block_kernel(nc, *args)
    r = _run(nc, [arrays], core_ids=[0])
    got = tuple(r.results[0][f"out_{i}_dram"] for i in range(len(_OUTS)))
    return got[0]
```

```python
from contextlib import ExitStack

import concourse.bass as bass
from concourse import mybir

ALU = mybir.AluOpType
ACT = mybir.ActivationFunctionType
AX = mybir.AxisListType
F32 = mybir.dt.float32
F32R = mybir.dt.float32r
BF16 = mybir.dt.bfloat16
I32 = mybir.dt.int32
P = 128
BANK = 512


class Sem:

    def __init__(self, nc, ctx, name):
        self.sem = ctx.enter_context(nc.semaphore(name))
        self.value = 0

    def up(self, ins, by=1):
        ins.then_inc(self.sem, by)
        self.value += by
        return (self, self.value)

    def dma(self, ins):
        return self.up(ins, 16)

    def later(self):
        self.value += 1
        return (self, self.value)


class Buf:

    def __init__(self, ap):
        self.ap = ap
        self.ready = ()
        self.free = ()


def moe_block_kernel(nc, x, ctx_in, g_xattn, g_ffn, Wq, bq, Wk, bk, Wv, bv, Wo, bo,
                     router_w, router_b, w1, b1, w2, b2, out):
    NB, SEQ, D = x.shape
    NKV, CK = ctx_in.shape[1:]
    E, _, FF = w1.shape
    H = 16
    DH = D // H
    TOK = NB * SEQ
    TOPK = 2
    CAP = -(-5 * TOK * TOPK // (4 * E))
    CLAMP = 10000.0
    SCALE = float(DH) ** -0.5
    EPS = 1e-5
    KD = D // P
    KC = CK // P
    NG = D // P
    HG = P // DH
    SUP = BANK
    TPS = SUP // P
    NS = TOK // SUP
    SPB = SEQ // SUP
    KEYS = H * NKV
    NCH = -(-KEYS // P)
    GK = HG * NKV
    HH = H // 2
    NF = FF // P
    ST = CAP // P
    FULL_RATE = 256
    GRAIN = 32
    WIDTHS = range(FULL_RATE, CAP + 1, GRAIN)
    CF = BANK // P
    NC = NF // CF
    NROW = E * ST
    FAR = 1.0e6
    assert CAP % P == 0 and CAP - FULL_RATE <= BANK and KD == CF == 4 and KEYS <= NCH * P and NROW <= P and GK <= BANK

    pairs = [[c for c in range(NCH) if c * P < (g + 1) * GK and (c + 1) * P > g * GK] for g in range(NG)]
    pair_at = {}
    for g in range(NG):
        for c in pairs[g]:
            pair_at[c, g] = len(pair_at)

    pe, act, dve, pool, sp = nc.tensor, nc.scalar, nc.vector, nc.gpsimd, nc.sync
    x_rows = x.rearrange("b s d -> (b s) d")
    out_rows = out.rearrange("b s d -> (b s) d")
    x_sup = x_rows.rearrange("(s t p) d -> s p t d", p=P, t=TPS)
    out_sup = out_rows.rearrange("(s t p) d -> s p t d", p=P, t=TPS)
    normed = nc.dram_tensor("normed_rows", (TOK, D), F32).ap()
    normed_sup = normed.rearrange("(s t p) d -> s p t d", p=P, t=TPS)

    top = ExitStack()
    with top:
        sems = {}

        def S(name):
            if name not in sems:
                sems[name] = Sem(nc, top, name)
            return sems[name]

        seen = {}

        def unseen(eng, *events):
            news = []
            for event in events:
                if event is None:
                    continue
                if isinstance(event, list) or (event and not isinstance(event[0], Sem)) or event == ():
                    news += unseen(eng, *event)
                    continue
                sem, value = event
                if seen.get((id(eng), id(sem)), 0) < value:
                    seen[id(eng), id(sem)] = value
                    news.append(event)
            return news

        def wait(eng, *events):
            for sem, value in unseen(eng, *events):
                eng.wait_ge(sem.sem, value)

        def sb(ctx, name, shape, dt=F32):
            return ctx.enter_context(nc.sbuf_tensor(name, shape, dt))

        ring_a = [top.enter_context(nc.psum_tensor(f"ring_a{i}", [P, BANK], F32)) for i in range(2)]
        pair = [top.enter_context(nc.psum_tensor(f"pair{i}", [P, 2, BANK], F32)) for i in range(2)]
        ring_b = [top.enter_context(nc.psum_tensor(f"ring_b{i}", [P, BANK], F32)) for i in range(2)]
        bank_a = [Buf(t) for t in ring_a]
        bank_b = [Buf(t) for t in ring_b]
        score_pair = [Buf(t) for t in pair]
        turn = {"a": 0, "b": 0, "s": 0, "m": 0}

        def take(name, banks):
            turn[name] += 1
            return banks[(turn[name] - 1) % len(banks)]

        ident = sb(top, "ident", [P, P])
        ones_f = sb(top, "ones_f", [P, P])
        tanh_g = sb(top, "tanh_g", [P, 2])
        bias_cols = sb(top, "bias_cols", [P, 2 * KD])
        b1_cols = sb(top, "b1_cols", [P, E * NF])
        router_wT = sb(top, "router_wT", [P, KD, E])
        router_b_col = sb(top, "router_b_col", [E, 1])
        bo_rows = sb(top, "bo_rows", [P, D])
        mean_v = sb(top, "mean_v", [P, NG, NB])
        nan_sums = sb(top, "nan_sums", [P, 2 * TOK // P])
        nan_total = sb(top, "nan_total", [P, 1])
        no_nan = sb(top, "no_nan", [P, 1])
        keep_mask = sb(top, "keep_mask", [P, 1], I32)
        drop_mask = sb(top, "drop_mask", [P, 1], I32)
        mean_bits = sb(top, "mean_bits", [P, NG, NB], I32)
        stats = sb(top, "stats", [P, 2, TPS, 6])
        mean_var = sb(top, "mean_var", [P, TPS, 2])
        var_eps = sb(top, "var_eps", [P, TPS])
        half_bits = sb(top, "half_bits", [P, TPS], I32)
        rstd = sb(top, "rstd", [P, TPS])
        newton = sb(top, "newton", [P, TPS])
        shift = sb(top, "shift", [P, TPS])
        NSM = 4
        smax = [sb(top, f"smax{i}", [P, HH]) for i in range(NSM)]
        ssum = [sb(top, f"ssum{i}", [P, HH]) for i in range(NSM)]
        slot_token = sb(top, "slot_token", [P, NROW], I32)
        slot_gate = sb(top, "slot_gate", [P, NROW])
        choices = sb(top, "choices", [1, E], I32)

        lay1 = ExitStack()
        Wq_hi = sb(lay1, "Wq_hi", [P, KD, D], F32R)
        Wq_lo = sb(lay1, "Wq_lo", [P, KD, D], F32R)
        k_block = sb(lay1, "k_block", [P, NB, NG, GK])
        v_pack = sb(lay1, "v_pack", [P, NB, len(pair_at), P])
        xT_hi = Buf(sb(lay1, "xT_hi", [P, KD, SUP], F32R))
        xT_lo = Buf(sb(lay1, "xT_lo", [P, KD, SUP], F32R))
        qT = [Buf(sb(lay1, f"qT{i}", [P, NG, SUP])) for i in range(2)]
        NP = 3
        probs = [Buf(sb(lay1, f"probs{i}", [P, NCH * P])) for i in range(NP)]
        pT = [Buf(sb(lay1, f"pT{i}", [P, NCH, 2 * P])) for i in range(2)]
        lay12 = ExitStack()
        raw = ExitStack()
        Wq_raw = sb(raw, "Wq_raw", [P, KD, D])
        Wo_raw = sb(raw, "Wo_raw", [P, KD, D])
        Wk_sb = sb(raw, "Wk_sb", [P, KC, D])
        Wv_sb = sb(raw, "Wv_sb", [P, KC, D])
        ctx_sb = sb(raw, "ctx_sb", [NKV, NB, CK])
        ctxT = sb(raw, "ctxT", [P, KC, NB * NKV])
        v_sb = sb(raw, "v_sb", [NKV, NB, D])
        inv_keys = sb(raw, "inv_keys", [P, 1])
        bias_rows = sb(raw, "bias_rows", [2 * KD, P])
        b1_rows = sb(raw, "b1_rows", [P, E * NF // P, P])
        bv_row = sb(raw, "bv_row", [1, D])
        bo_row = sb(raw, "bo_row", [1, D])
        rw_rows = sb(raw, "rw_rows", [E, D])
        gate_in = sb(raw, "gate_in", [P, 2])
        raw.close()
        attn_out = sb(lay12, "attn_out", [P, NG, TOK])
        xs = [Buf(sb(lay12, f"x_sup{i}", [P, TPS, D])) for i in range(2)]
        Wo_hi = sb(lay12, "Wo_hi", [P, KD, D], F32R)
        Wo_lo = sb(lay12, "Wo_lo", [P, KD, D], F32R)
        lay12.close()
        lay1.close()
        lay3 = top
        w_raw = [(Buf(sb(lay3, f"w1_raw{i}", [P, KD, BANK])), Buf(sb(lay3, f"w2_raw{i}", [P, CF, D])))
                 for i in range(2)]
        xg = Buf(sb(lay3, "gathered", [P, ST, D]))
        lay2 = ExitStack()
        NA = 4
        ao_hi = [Buf(sb(lay2, f"ao_hi{i}", [P, NG, P], F32R)) for i in range(NA)]
        ao_lo = [Buf(sb(lay2, f"ao_lo{i}", [P, NG, P], F32R)) for i in range(NA)]
        xn2 = [Buf(sb(lay2, f"xn2_{i}", [P, TPS, D])) for i in range(2)]
        xn2T = Buf(sb(lay2, "xn2T", [P, KD, SUP]))
        logitT = Buf(sb(lay2, "logitT", [E, SUP]))
        BT = 2 * TPS
        logits = sb(lay2, "logits", [P, BT, E])
        rest = sb(lay2, "rest", [P, BT, E])
        hit = sb(lay2, "hit", [P, BT, E])
        place = sb(lay2, "place", [P, BT, E])
        one_hot = sb(lay2, "one_hot", [P, TOPK, BT, E])
        chosen = sb(lay2, "chosen", [P, BT, E], BF16)
        taken = sb(lay2, "taken", [P, BT + 1, E], BF16)
        best = sb(lay2, "best", [P, TOPK, BT])
        best_no = sb(lay2, "best_no", [P, TOPK, BT])
        prior = sb(lay2, "prior", [P, TOPK, BT, E])
        pos = sb(lay2, "pos", [P, TOPK, BT])
        slot_hi = sb(lay2, "slot_hi", [P, TOPK, BT])
        slot_lo = sb(lay2, "slot_lo", [P, TOPK, BT])
        kept = sb(lay2, "kept", [P, TOPK, BT])
        away = sb(lay2, "away", [P, TOPK, BT])
        gap = sb(lay2, "gap", [P, BT])
        gexp = sb(lay2, "gexp", [P, BT])
        gden = sb(lay2, "gden", [P, BT])
        gate = sb(lay2, "gate", [P, TOPK, BT])
        TG = TPS
        at_lo = [Buf(sb(lay2, f"at_lo{i}", [P, TG, P])) for i in range(2)]
        at_eq = [Buf(sb(lay2, f"at_eq{i}", [P, TG, NROW])) for i in range(2)]
        at_hi = [Buf(sb(lay2, f"at_hi{i}", [P, TG, 2, NROW])) for i in range(2)]
        ones_b = sb(lay2, "ones_b", [P, P], BF16)
        before = sb(lay2, "before", [P, P], BF16)
        expert_no = sb(lay2, "expert_no", [P, E])
        expert_no_far = sb(lay2, "expert_no_far", [P, E])
        token_no = sb(lay2, "token_no", [P, TOK // P])
        row_no = sb(lay2, "row_no", [P, P])
        empty = sb(lay2, "empty", [P, NROW])
        lay2.close()
        w_split = [[Buf(sb(lay3, f"{n}_{h}{i}", [P, CF, BANK], F32R)) for n in ("w1", "w2") for h in ("hi", "lo")]
                   for i in range(2)]
        xgT = [(Buf(sb(lay3, f"xgT_hi{i}", [P, KD, CAP], F32R)), Buf(sb(lay3, f"xgT_lo{i}", [P, KD, CAP], F32R)))
               for i in range(2)]
        h_full = [Buf(sb(lay3, f"h_full{i}", [P, CAP])) for i in range(2)]
        NH = 4
        h_hi = [Buf(sb(lay3, f"h_hi{i}", [P, CAP], F32R)) for i in range(NH)]
        h_lo = [Buf(sb(lay3, f"h_lo{i}", [P, CAP], F32R)) for i in range(NH)]
        b2_rows = [Buf(sb(lay3, f"b2_rows{i}", [P, D])) for i in range(2)]
        y = Buf(sb(lay3, "y", [P, ST, D]))

        def row(v):
            return v.rearrange("(a n) -> a n", a=1)

        def bc(ap, shape, dim=None):
            return ap.to_broadcast(shape)

        def load_x(s):
            b = xs[s % NS % 2]
            wait(sp, b.free)
            b.ready = S(f"load_x{s % NS % 2}").dma(sp.dma_start(b.ap[:], x_sup[s % NS]))

        load_x(0)
        ctx_loaded = S("load_ctx").dma(act.dma_start(ctx_sb[:], ctx_in.rearrange("b j c -> j b c")))
        for dst, src in ((bias_rows[0:KD, :], bq.rearrange("(k p) -> k p", p=P)),
                         (bias_rows[KD:2 * KD, :], bk.rearrange("(k p) -> k p", p=P)),
                         (rw_rows[:], router_w),
                         (b1_rows[:], b1.rearrange("e (f p) -> (e f) p", p=P).rearrange("(r q) p -> q r p", q=P))):
            to_turn = S("load_bias").dma(act.dma_start(dst, src))
        wk_in = S("load_wk").dma(sp.dma_start(Wk_sb[:], Wk.rearrange("(k p) n -> p k n", p=P)))
        wq_in = S("load_wq").dma(sp.dma_start(Wq_raw[:], Wq.rearrange("(k p) n -> p k n", p=P)))
        for dst, src in ((bv_row[:], row(bv)), (bo_row[:], row(bo)),
                         (router_b_col[:], router_b.rearrange("(e a) -> e a", a=1)),
                         (gate_in[:, 0:1], g_xattn.partition_broadcast(P)),
                         (gate_in[:, 1:2], g_ffn.partition_broadcast(P))):
            rows_loaded = S("load_rows").dma(sp.dma_start(dst, src))
        wv_in = S("load_wv").dma(sp.dma_start(Wv_sb[:], Wv.rearrange("(k p) n -> p k n", p=P)))
        load_x(1)
        wo_in = S("load_wo").dma(sp.dma_start(Wo_raw[:], Wo.rearrange("(k p) n -> p k n", p=P)))

        const = S("pool_const")
        wait(pool, const.up(pool.memset(ident[:], 0.0)))
        const.up(pool.affine_select(out=ident[:], in_=ident[:], compare_op=ALU.not_equal, fill=1.0, base=0,
                                    pattern=[[-1, P]], channel_multiplier=1))
        const.up(pool.memset(inv_keys[:], 1.0 / NKV))
        ident_done = const.up(pool.memset(ones_f[:], 1.0))
        k_clear = const.up(pool.memset(k_block[:], 0.0))
        v_clear = const.up(pool.memset(v_pack[:], 0.0))
        for b in range(NP):
            const_done = const.up(pool.memset(probs[b].ap[:, KEYS:NCH * P], 0.0))

        def late_constants():
            wait(pool, attn_done)
            wait(pool, const.up(pool.memset(before[:], 1.0)))
            const.up(pool.affine_select(out=before[:], in_=before[:], compare_op=ALU.is_gt, fill=0.0, base=0,
                                        pattern=[[1, P]], channel_multiplier=-1))
            const.up(pool.memset(ones_b[:], 1.0))
            for dst, base, pattern, rows in ((expert_no, 0, [[1, E]], 0), (expert_no_far, 100, [[1, E]], 0),
                                             (row_no, 0, [[1, P]], 0), (token_no, 1, [[P, TOK // P]], 1)):
                done = const.up(pool.iota(dst[:], pattern=pattern, base=base, channel_multiplier=rows,
                                          allow_small_or_imprecise_dtypes=True))
            return done

        def evac_copy(eng, dst, src, sem):
            if eng is act:
                return sem.up(act.activation(dst, src, ACT.Copy))
            return sem.up(eng.tensor_copy(dst, src))

        def chained(sem, *lists):
            lists = [iter(steps) for steps in lists]
            last = [(sem, sem.value) if sem.value else None] * len(lists)
            while lists:
                for i, emit in enumerate([next(steps, None) for steps in lists]):
                    if emit is None:
                        lists[i] = last[i] = None
                        continue
                    wait(dve, last[i])
                    last[i] = sem.up(emit())
                    yield
                lists, last = [x for x in lists if x], [x for x in last if x]

        chains = []
        deferred = []

        def emit_deferred():
            while deferred:
                deferred.pop(0)()

        STUCK = "waits for a deferred product"

        def draw(n):
            for _ in range(n):
                if not chains:
                    return None
                c = chains.pop(0)
                said = next(c, chains)
                if said is not chains:
                    chains.append(c)
            return said

        def finish(c, alone=False):
            if alone and c in chains:
                chains.remove(c)
            while c in chains:
                if draw(1) is STUCK:
                    emit_deferred()
            for said in c:
                if said is STUCK:
                    emit_deferred()

        ln = S("dve_ln")

        def stats_of(src, i, t):
            return ln.up(dve.bn_stats(stats[:, i, t, :], src[:, t, :]))

        def rstd_steps(i):
            def aggregate():
                for t in range(TPS - 1):
                    ln.up(dve.bn_aggr(mean_var[:, t, :], stats[:, i, t, :]))
                return dve.bn_aggr(mean_var[:, TPS - 1, :], stats[:, i, TPS - 1, :])
            yield aggregate
            yield lambda: dve.tensor_scalar(var_eps[:], mean_var[:, :, 1:2].rearrange("p t a -> p (t a)"), EPS, None,
                                            ALU.add)
            yield lambda: dve.tensor_scalar(half_bits[:], var_eps[:].bitcast(I32), 1, None, ALU.logical_shift_right)
            yield lambda: dve.tensor_scalar(rstd[:].bitcast(I32), half_bits[:], -1.0, float(0x5F3759DF), ALU.mult,
                                            ALU.add)
            for _ in range(3):
                yield lambda: dve.tensor_tensor(newton[:], rstd[:], var_eps[:], ALU.mult)
                yield lambda: dve.scalar_tensor_tensor(out=newton[:], in0=newton[:], scalar=-0.5, in1=rstd[:],
                                                       op0=ALU.mult, op1=ALU.mult)
                yield lambda: dve.scalar_tensor_tensor(out=rstd[:], in0=newton[:], scalar=1.5, in1=rstd[:],
                                                       op0=ALU.add, op1=ALU.mult)

        def normalise(dst, src):
            wait(dve, (ln, ln.value))
            for t in range(TPS):
                ln.up(dve.tensor_scalar(dst[:, t, :], src[:, t, :], mean_var[:, t, 0:1], rstd[:, t:t + 1],
                                        ALU.subtract, ALU.mult))
                yield

        def norm_x(s):
            b = xs[s % 2]
            wait(dve, b.ready)
            for t in range(TPS):
                stats_of(b.ap, s % 2, t)
                yield
            yield from chained(ln, rstd_steps(s % 2))
            yield from normalise(b.ap, b.ap)
            b.ready = (ln, ln.value)

        def turn_x(s, k):
            b = xs[s % 2]
            bank = take("a", bank_a)
            wait(pe, bank.free, b.ready)
            for t in range(TPS):
                ins = pe.transpose(bank.ap[:, t * P:(t + 1) * P], b.ap[:, t, k * P:(k + 1) * P], ident[:])
            turned = S("pe_turn_x").up(ins)
            wait(act, turned, xT_hi.free)
            hi = S("act_xT").up(act.activation(xT_hi.ap[:, k, :], bank.ap[:], ACT.Copy))
            wait(dve, turned, hi, xT_lo.free)
            lo = S("dve_xT").up(dve.tensor_tensor(xT_lo.ap[:, k, :], bank.ap[:], xT_hi.ap[:, k, :], ALU.subtract))
            bank.free = (hi, lo)
            xT_hi.ready, xT_lo.ready = hi, lo
            if k == KD - 1:
                b.free = turned

        def split_products(acc, ks, w_hi, w_lo, m_hi, m_lo, first=True, last=True):
            ins = None
            for i, k in enumerate(ks):
                for j, (w, m) in enumerate(((w_hi, m_lo), (w_lo, m_hi), (w_hi, m_hi))):
                    ins = pe.matmul(acc, w(k), m(k), start=first and i == 0 and j == 0,
                                    stop=last and i == len(ks) - 1 and j == 2)
            return ins

        def project_q(s, g):
            bank = take("a", bank_a)
            wait(pe, bank.free, xT_hi.ready, xT_lo.ready, wq_done)
            c = slice(g * P, (g + 1) * P)
            ins = split_products(bank.ap[:], range(KD), lambda k: Wq_hi[:, k, c], lambda k: Wq_lo[:, k, c],
                                 lambda k: xT_hi.ap[:, k, :], lambda k: xT_lo.ap[:, k, :])
            q_done = S("pe_q").up(ins)
            if g == NG - 1:
                xT_hi.free = xT_lo.free = q_done
            q = qT[s % 2]
            wait(act, q_done, q.free, cols_done)
            q.ready = bank.free = S("act_q").up(act.activation(q.ap[:, g, :], bank.ap[:], ACT.Identity,
                                                               bias=bias_cols[:, g:g + 1]))

        softmax = {}

        def scores(u):
            tile, half = divmod(u, 2)
            s, t = divmod(tile, TPS)
            b = s // SPB
            pr = probs[tile % NP]
            sc = take("s", score_pair)
            wait(pe, sc.free, qT[s % 2].ready, k_done)
            for j in range(2):
                ins = pe.matmul(sc.ap[:, j, 0:GK], qT[s % 2].ap[:, 2 * half + j, t * P:(t + 1) * P],
                                k_block[:, b, 2 * half + j, :], start=True, stop=True)
            scored = S("pe_scores").up(ins)
            if u % (2 * TPS) == 2 * TPS - 1:
                qT[s % 2].free = scored
            sc3 = sc.ap[:, :, 0:GK].rearrange("p j (a n) -> p j a n", n=NKV)
            i = u % NSM
            n = S("dve_softmax")
            d = pr.ap[:, half * HH * NKV:(half + 1) * HH * NKV]
            wait(act, scored, pr.free)
            nan_seen = S("act_nan").up(act.activation(d.rearrange("p (j n) -> p j n", j=2), sc.ap[:, :, 0:GK],
                                                      ACT.Tanh, accum_out=nan_sums[:, u:u + 1]))
            mx = smax[i]
            draw(1)
            wait(dve, nan_seen)
            clipped = n.up(dve.tensor_scalar(d.rearrange("p (j a n) -> p j a n", j=2, n=NKV), sc3, -CLAMP, CLAMP,
                                             ALU.max, ALU.min))
            draw(2)
            wait(dve, clipped, softmax.get(u - NSM, {}).get("all"))
            d3 = d.rearrange("p (a n) -> p a n", n=NKV)
            greatest = n.up(dve.tensor_reduce(mx[:], d3, AX.X, ALU.max))
            sc.free = clipped
            wait(pool, greatest)
            mxb = mx[:].rearrange("p (a o) -> p a o", o=1).to_broadcast([P, HH, NKV])
            softmax[u] = {"less": S("pool_less").up(pool.tensor_tensor(d3, d3, mxb, ALU.subtract))}

        def normal_probs(u):
            tile, half = divmod(u, 2)
            pr = probs[tile % NP]
            d = pr.ap[:, half * HH * NKV:(half + 1) * HH * NKV]
            d3 = d.rearrange("p (a n) -> p a n", n=NKV)
            sm = ssum[u % NSM]
            wait(act, softmax[u]["less"])
            draw(1)
            e = S("act_exp").up(act.activation(d, d, ACT.Exp))
            wait(dve, e)
            n = S("dve_softmax")
            total = n.up(dve.tensor_reduce(sm[:], d3, AX.X, ALU.add))
            draw(1)
            wait(dve, total)
            r = n.up(dve.reciprocal(sm[:], sm[:]))
            wait(pool, r, e)
            smb = sm[:].rearrange("p (a o) -> p a o", o=1).to_broadcast([P, HH, NKV])
            pr.ready = S("pool_probs").up(pool.tensor_tensor(d3, d3, smb, ALU.mult))
            softmax[u]["all"] = (pr.ready, r)

        def turn_probs(tile, part):
            pr, dst = probs[tile % NP], pT[tile // 2 % 2]
            t = tile % 2
            for c0 in (range(0, 8, 4) if part == 0 else range(8, NCH, 4)):
                cs = range(c0, min(c0 + 4, NCH))
                bank = take("b", bank_b)
                wait(pe, bank.free, pr.ready, const_done)
                for c in cs:
                    ins = pe.transpose(bank.ap[:, (c - c0) * P:(c - c0 + 1) * P], pr.ap[:, c * P:(c + 1) * P], ident[:])
                turned = S("pe_turn_p").up(ins)
                eng = dve if c0 == 4 else act
                wait(eng, turned, dst.free)
                bank.free = evac_copy(eng, dst.ap[:, cs[0]:cs[-1] + 1, t * P:(t + 1) * P],
                                      bank.ap[:, 0:len(cs) * P].rearrange("p (c n) -> p c n", n=P),
                                      S("act_pT" if eng is act else "dve_pT"))
                dst.ready = (*dst.ready, bank.free)
            pr.free = turned

        def attend(two, g):
            b = two * 2 // (TPS * SPB)
            src = pT[two % 2]
            bank = take("a", bank_a)
            wait(pe, bank.free, src.ready, packed)
            for c in pairs[g]:
                ins = pe.matmul(bank.ap[:, 0:2 * P], v_pack[:, b, pair_at[c, g], :], src.ap[:, c, :],
                                start=c == pairs[g][0], stop=c == pairs[g][-1])
            done = S("pe_attend").up(ins)
            wait(act, done, raw_free)
            bank.free = S("act_attn").up(act.activation(attn_out[:, g, two * 2 * P:(two + 1) * 2 * P],
                                                        bank.ap[:, 0:2 * P], ACT.Copy))
            if g == NG - 1:
                src.ready = ()
                src.free = done
            return bank.free

        setup_pe, setup_dve, setup_act = S("pe_setup"), S("dve_setup"), S("act_setup")
        wait(pe, ctx_loaded, ident_done)
        for b in range(NB):
            bank = take("a", bank_a)
            for k in range(KC):
                ins = pe.transpose(bank.ap[:, k * NKV:(k + 1) * NKV], ctx_sb[:, b, k * P:(k + 1) * P],
                                   ident[0:NKV, 0:NKV])
            wait(act, setup_pe.up(ins))
            bank.free = ctx_turned = setup_act.up(act.activation(
                ctxT[:, :, b * NKV:(b + 1) * NKV], bank.ap[:, 0:KC * NKV].rearrange("p (k j) -> p k j", j=NKV),
                ACT.Copy))
        wait(pe, wk_in, ctx_turned)
        k_bank = score_pair[0]
        for g in range(NG):
            at = k_bank.ap[:, g // 2, g % 2 * NB * NKV:(g % 2 + 1) * NB * NKV]
            for k in range(KC):
                ins = pe.matmul(at, Wk_sb[:, k, g * P:(g + 1) * P], ctxT[:, k, :], start=k == 0, stop=k == KC - 1)
        k_made = setup_pe.up(ins)
        finish(norm_x(0))
        wait(act, wq_in)
        wq_hi_done = setup_act.up(act.activation(Wq_hi[:], Wq_raw[:], ACT.Copy))
        wait(dve, wq_in, wq_hi_done)
        wq_done = setup_dve.up(dve.tensor_tensor(Wq_lo[:], Wq_raw[:], Wq_hi[:], ALU.subtract))
        for k in range(KD):
            turn_x(0, k)
        bank = take("a", bank_a)
        wait(pe, bank.free, to_turn)
        pe.transpose(bank.ap[:, 0:2 * KD], bias_rows[:], ident[0:2 * KD, 0:2 * KD])
        for k in range(KD):
            pe.transpose(bank.ap[:, 16 + k * E:16 + (k + 1) * E], rw_rows[:, k * P:(k + 1) * P], ident[0:E, 0:E])
        for r in range(E * NF // P):
            ins = pe.transpose(bank.ap[:, 128 + r * P:128 + (r + 1) * P], b1_rows[:, r, :], ident[:])
        wait(act, setup_pe.up(ins))
        setup_act.up(act.activation(bias_cols[:], bank.ap[:, 0:2 * KD], ACT.Copy))
        setup_act.up(act.activation(router_wT[:].rearrange("p k e -> p (k e)"), bank.ap[:, 16:16 + KD * E], ACT.Copy))
        cols_done = setup_act.up(act.activation(b1_cols[:], bank.ap[:, 128:128 + E * NF], ACT.Copy))
        bank.free = cols_done
        wait(act, rows_loaded)
        tanh_done = S("act_tanh").up(act.activation(tanh_g[:], gate_in[:], ACT.Tanh))

        def make_v(b):
            bank = take("b", bank_b)
            wait(pe, bank.free, wv_in, rows_loaded)
            for k in range(KC):
                pe.matmul(bank.ap[0:NKV, :], ctxT[:, k, b * NKV:(b + 1) * NKV], Wv_sb[:, k, :], start=k == 0,
                          stop=False)
            ins = pe.matmul(bank.ap[0:NKV, :], ones_f[0:1, 0:NKV], bv_row[:], start=False, stop=True)
            wait(act, setup_pe.up(ins))
            bank.free = setup_act.up(act.activation(v_sb[:, b, :], bank.ap[0:NKV, :], ACT.Copy))
            return bank.free

        def block_k(g):
            wait(dve, k_made, cols_done, k_clear)
            at = k_bank.ap[:, g // 2, g % 2 * NB * NKV:(g % 2 + 1) * NB * NKV]
            for a in range(HG):
                q = slice(a * DH, (a + 1) * DH)
                k_bank.free = setup_dve.up(dve.tensor_scalar(
                    k_block[q, :, g, a * NKV:(a + 1) * NKV], at[q, :].rearrange("p (b j) -> p b j", j=NKV),
                    bias_cols[q, KD + g:KD + g + 1], SCALE, ALU.add, ALU.mult))
                draw(1)
            return k_bank.free

        make_v(0)
        chains.append(norm_x(1))
        norm_1 = chains[0]
        for g in range(NG):
            project_q(0, g)
            k_done = block_k(g)
        load_x(2)
        v_done = make_v(1)
        pack = S("pack_v")
        wait(sp, v_done, v_clear)
        for h in range(H):
            g = h // HG
            for c in pairs[g]:
                lo, hi = max(h * NKV, c * P), min((h + 1) * NKV, (c + 1) * P)
                if lo < hi:
                    packed = pack.dma(sp.dma_start(
                        v_pack[lo - c * P:hi - c * P, :, pair_at[c, g], (h % HG) * DH:(h % HG + 1) * DH],
                        v_sb[lo - h * NKV:hi - h * NKV, :, h * DH:(h + 1) * DH]))
        guard = S("dve_guard")

        def look_for_nan():
            wait(dve, (S("act_nan"), S("act_nan").value))
            wait(pe, guard.up(dve.tensor_reduce(nan_total[:], nan_sums[:], AX.X, ALU.add)))
            bank = take("a", bank_a)
            wait(pe, bank.free)
            summed = S("pe_guard").up(pe.matmul(bank.ap[:, 0:1], ones_f[:], nan_total[:], start=True, stop=True))
            wait(dve, summed)
            wait(dve, guard.up(dve.tensor_copy(nan_total[:], bank.ap[:, 0:1])))
            bank.free = (guard, guard.value)
            wait(dve, guard.up(dve.tensor_tensor(no_nan[:], nan_total[:], nan_total[:], ALU.is_equal)))
            guard.up(dve.tensor_scalar(drop_mask[:], no_nan[:], 1.0, None, ALU.subtract))
            wait(dve, guard.up(dve.tensor_scalar(keep_mask[:], no_nan[:], -1.0, None, ALU.mult)))
            wait(dve, guard.up(dve.tensor_tensor(mean_bits[:].rearrange("p g b -> p (g b)"),
                                                 mean_v[:].bitcast(I32).rearrange("p g b -> p (g b)"),
                                                 drop_mask[:].to_broadcast([P, NG * NB]), ALU.bitwise_and)))

        def finish_setup():
            bank = take("b", bank_b)
            wait(pe, bank.free)
            wait(dve, setup_pe.up(pe.matmul(bank.ap[:], ones_f[0:1, :], bo_row[:], start=True, stop=True)), tanh_done)
            bank.free = setup_dve.up(dve.tensor_scalar(bo_rows[:], bank.ap[:], tanh_g[:, 0:1], None, ALU.mult))
            bank = take("b", bank_b)
            wait(pe, bank.free, v_done)
            for g in range(NG):
                for b in range(NB):
                    ins = pe.matmul(bank.ap[:, g * NB + b:g * NB + b + 1], v_sb[:, b, g * P:(g + 1) * P],
                                    inv_keys[0:NKV, :], start=True, stop=True)
            wait(dve, setup_pe.up(ins))
            mean_done = setup_dve.up(dve.tensor_copy(mean_v[:].rearrange("p g b -> p (g b)"), bank.ap[:, 0:NG * NB]))
            bank.free = mean_done
            wait(act, wo_in)
            wo_hi_done = setup_act.up(act.activation(Wo_hi[:], Wo_raw[:], ACT.Copy))
            wait(pool, wo_in, wo_hi_done)
            wo_done = S("pool_wo").up(pool.tensor_tensor(Wo_lo[:], Wo_raw[:], Wo_hi[:], ALU.subtract))
            return wo_done, mean_done

        finish(norm_1)
        UNITS = 2 * TPS
        units = UNITS * NS
        TURN, ATTEND = 5, 9
        project_at = {s: {0: 0, 2: 1, 4: 2, 6: 3} for s in range(1, NS)}
        project_at[1] = {1: 0, 3: 1, 5: 2, 6: 3}
        for u in range(units + ATTEND + 1):
            s, part = divmod(u, UNITS)
            turning = part == UNITS - 1 and s + 2 < NS
            if part == 0 and s + 2 < NS:
                norming = norm_x(s + 2)
                chains.append(norming)
            if turning:
                finish(norming)
                turn_x(s + 2, 0)
            if u < units:
                scores(u)
            if turning:
                turn_x(s + 2, 1)
            if u == 0:
                for k in range(KD):
                    turn_x(1, k)
                load_x(3)
            if 1 <= u <= units:
                normal_probs(u - 1)
            if u == 3:
                wo_done, mean_done = finish_setup()
                raw_free = (wq_done, wo_done, packed, mean_done)
            if u == units + 1:
                look_for_nan()
            if s + 1 < NS and part in project_at[s + 1]:
                project_q(s + 1, project_at[s + 1][part])
            if 0 <= u - ATTEND < units:
                attn_done = attend((u - ATTEND) // 4, (u - ATTEND) % 4)
            if turning:
                turn_x(s + 2, 2)
            if 0 <= u - TURN < units:
                turn_probs(*divmod(u - TURN, 2))
            if turning:
                turn_x(s + 2, 3)
                load_x(s + 4)
            draw(2)

        wait(dve, attn_done)
        with dve.If(dve.value_load(keep_mask[0:1, 0:1]) == 0):
            for s in range(NS):
                for g in range(NG):
                    bits = attn_out[:, g, s * SUP:(s + 1) * SUP].bitcast(I32)
                    dve.tensor_scalar(bits, bits, keep_mask[:, 0:1], mean_bits[:, g, s // SPB:s // SPB + 1],
                                      ALU.bitwise_and, ALU.bitwise_or)
        guarded = guard.up(dve.tensor_copy(nan_total[:], no_nan[:]))

        route = S("dve_route")
        stored = S("store_out")
        stored_norm = [S("store_normed0"), S("store_normed1")]
        route.up(dve.memset(taken[:, 0, :], 0.0))
        table_bank = Buf(pair[1][:, 1, :])
        table_bank.free = (score_pair[0].free, score_pair[1].free)
        logit_bank, logit_turn_bank, count_bank = (Buf(pair[0][:, 0, :]), Buf(pair[0][:, 1, :]), Buf(pair[1][:, 0, :]))
        for b in (logit_bank, logit_turn_bank, count_bank):
            b.free = table_bank.free
        NT = TOK // P

        def split_attn(v):
            hi, lo = ao_hi[v % NA], ao_lo[v % NA]
            src = attn_out[:, :, v * P:(v + 1) * P]
            wait(act, guarded, hi.free)
            hi.ready = S("act_ao").up(act.activation(hi.ap[:], src, ACT.Copy))
            wait(pool, hi.ready, lo.free)
            lo.ready = S("pool_ao").up(pool.tensor_tensor(lo.ap[:], src, hi.ap[:], ALU.subtract))

        based = {}

        def add_bo(v):
            s, t = divmod(v, TPS)
            b = xs[s % 2]
            wait(pool, b.ready)
            based[v] = S("pool_base").up(pool.tensor_tensor(b.ap[:, t, :], b.ap[:, t, :], bo_rows[:], ALU.add))

        def project_out(v):
            bank = take("a", bank_a)
            hi, lo = ao_hi[v % NA], ao_lo[v % NA]
            wait(pe, bank.free, hi.ready, lo.ready, wo_done)
            ins = split_products(bank.ap[:], range(KD), lambda k: hi.ap[:, k, :], lambda k: lo.ap[:, k, :],
                                 lambda k: Wo_hi[:, k, :], lambda k: Wo_lo[:, k, :])
            hi.free = lo.free = S("pe_y").up(ins)
            return bank

        def residual(v, bank):
            s, t = divmod(v, TPS)
            b, r = xs[s % 2], xn2[s % 2]
            wait(dve, (S("pe_y"), S("pe_y").value), based[v], r.free)
            added = S("dve_resid").up(dve.scalar_tensor_tensor(
                out=r.ap[:, t, :], in0=bank.ap[:], scalar=tanh_g[:, 0:1], in1=b.ap[:, t, :], op0=ALU.mult,
                op1=ALU.add))
            bank.free = added
            draw(2)
            wait(dve, added)
            stats_of(r.ap, s % 2, t)
            if t == TPS - 1:
                b.free = added
                wait(sp, added)
                r.stored = stored.dma(sp.dma_start(out_sup[s], r.ap[:]))
                if s + 2 < NS:
                    load_x(s + 2)

        def norm_steps(s):
            wait(dve, xn2[(s + 1) % 2].ready)
            yield from chained(ln, rstd_steps(s % 2))
            yield from chained(ln, [lambda: dve.scalar_tensor_tensor(
                out=shift[:], in0=mean_var[:, :, 0:1].rearrange("p t a -> p (t a)"), scalar=-1.0, in1=rstd[:],
                op0=ALU.mult, op1=ALU.mult)])

        def norm_rows(s):
            n = xn2[s % 2]
            wait(act, (ln, ln.value), n.stored)
            for t in range(TPS):
                n.ready = S("act_norm").up(act.activation(n.ap[:, t, :], n.ap[:, t, :], ACT.Identity,
                                                          bias=shift[:, t:t + 1], scale=rstd[:, t:t + 1]))
            wait(sp, n.ready)
            n.free = (stored_norm[s % 2].dma(sp.dma_start(normed_sup[s], n.ap[:])),)

        def turn_rows_out(s, k):
            n = xn2[s % 2]
            bank = take("b", bank_b)
            wait(pe, bank.free, n.ready)
            for t in range(TPS):
                ins = pe.transpose(bank.ap[:, t * P:(t + 1) * P], n.ap[:, t, k * P:(k + 1) * P], ident[:])
            turned = S("pe_turn_n").up(ins)
            wait(act, turned, xn2T.free)
            xn2T.ready = bank.free = S("act_nT").up(act.activation(xn2T.ap[:, k, :], bank.ap[:], ACT.Copy))
            if k == KD - 1:
                n.free = (*n.free, turned)

        def router(s):
            wait(pe, logit_bank.free, xn2T.ready)
            for k in range(KD):
                ins = pe.matmul(logit_bank.ap[0:E, :], router_wT[:, k, :], xn2T.ap[:, k, :], start=k == 0,
                                stop=k == KD - 1)
            xn2T.free = S("pe_router").up(ins)
            wait(act, xn2T.free, logitT.free)
            logitT.ready = logit_bank.free = S("act_logit").up(act.activation(
                logitT.ap[:], logit_bank.ap[0:E, :], ACT.Identity, bias=router_b_col[:]))

        def turn_logits(s, at):
            wait(pe, logitT.ready, logit_turn_bank.free)
            for t in range(TPS):
                ins = pe.transpose(logit_turn_bank.ap[:, t * E:(t + 1) * E], logitT.ap[:, t * P:(t + 1) * P],
                                   ident[0:E, 0:E])
            logitT.free = S("pe_router").up(ins)
            wait(dve, logitT.free, (route, route.value))
            logit_turn_bank.free = route.up(dve.tensor_copy(
                logits[:, at:at + TPS, :].rearrange("p t e -> p (t e)"), logit_turn_bank.ap[:, 0:TPS * E]))

        table_products, groups_made = [0], [0]
        gates_read = [None]

        def add_to_table(lo, hi, *made):
            wait(pe, *made, table_bank.free)
            for t in range(TG):
                table_products[0] += 1
                ins = pe.matmul(table_bank.ap[:, 0:2 * NROW], lo.ap[:, t, :],
                                hi.ap[:, t, :, :].rearrange("p c r -> p (c r)"),
                                start=table_products[0] == 1, stop=table_products[0] == TOPK * NT)
            lo.free = hi.free = S("pe_table").up(ins)

        def route_batch(v0, nt):
            def over_e(ap):
                return ap.rearrange("p (t o) -> p t o", o=1).to_broadcast([P, nt, E])

            def over_t(ap):
                return ap.rearrange("p (o e) -> p o e", o=1).to_broadcast([P, nt, E])

            T = slice(0, nt)
            oh = [one_hot[:, k, T, :] for k in range(TOPK)]

            def choose():
                for k, src in enumerate((logits[:, T, :], rest[:, T, :])):
                    yield lambda: dve.tensor_reduce(best[:, k, T], src, AX.X, ALU.max)
                    yield lambda: dve.tensor_tensor(hit[:, T, :], src, over_e(best[:, k, T]), ALU.is_equal)
                    yield lambda: dve.scalar_tensor_tensor(out=place[:, T, :], in0=hit[:, T, :], scalar=-100.0,
                                                           in1=over_t(expert_no_far[:]), op0=ALU.mult, op1=ALU.add)
                    yield lambda: dve.tensor_reduce(best_no[:, k, T], place[:, T, :], AX.X, ALU.min)
                    yield lambda: dve.tensor_tensor(oh[k], over_t(expert_no[:]), over_e(best_no[:, k, T]),
                                                    ALU.is_equal)
                    if k == 0:
                        yield lambda: dve.scalar_tensor_tensor(out=rest[:, T, :], in0=oh[0], scalar=-3.0e38,
                                                               in1=logits[:, T, :], op0=ALU.mult, op1=ALU.add)
                yield lambda: dve.tensor_tensor(chosen[:, T, :], oh[0], oh[1], ALU.add)
                for t in range(nt):
                    yield lambda: dve.tensor_tensor(taken[:, t + 1, :], taken[:, t, :], chosen[:, t, :], ALU.add)
                yield lambda: dve.tensor_tensor(gap[:, T], best[:, 1, T], best[:, 0, T], ALU.subtract)

            wait(dve, constants_done)
            yield from chained(route, choose())
            chosen_all = (route, route.value)
            counted = []

            def count():
                wait(pe, chosen_all, count_bank.free)
                acc = count_bank.ap[:, 0:nt * E]
                pe.matmul(acc, before[:], chosen[:, T, :].rearrange("p t e -> p (t e)"), start=True, stop=False)
                counted.append(S("pe_count").up(pe.matmul(
                    acc, ones_b[:], taken[:, T, :].rearrange("p t e -> p (t e)"), start=False, stop=True)))

            deferred.append(count)
            wait(act, chosen_all)
            odds = S("act_gate").up(act.activation(gexp[:, T], gap[:, T], ACT.Exp))
            while not counted:
                yield STUCK

            def place_them():
                yield lambda: dve.tensor_tensor(
                    prior[:, :, T, :], count_bank.ap[:, 0:nt * E].rearrange("p (o t e) -> p o t e", o=1, e=E)
                    .to_broadcast([P, TOPK, nt, E]), one_hot[:, :, T, :], ALU.mult)
                yield lambda: dve.tensor_reduce(pos[:, :, T], prior[:, :, T, :], AX.X, ALU.add)
                yield lambda: dve.tensor_scalar(kept[:, :, T], pos[:, :, T], float(CAP), None, ALU.is_lt)
                yield lambda: dve.tensor_scalar(away[:, :, T], kept[:, :, T], -FAR, FAR, ALU.mult, ALU.add)
                yield lambda: dve.tensor_scalar(slot_hi[:, :, T], pos[:, :, T], float(P), None, ALU.is_ge)
                for m in range(2, ST):
                    yield lambda: dve.scalar_tensor_tensor(out=slot_hi[:, :, T], in0=pos[:, :, T],
                                                           scalar=float(m * P), in1=slot_hi[:, :, T], op0=ALU.is_ge,
                                                           op1=ALU.add)
                yield lambda: dve.scalar_tensor_tensor(out=slot_lo[:, :, T], in0=slot_hi[:, :, T], scalar=-float(P),
                                                       in1=pos[:, :, T], op0=ALU.mult, op1=ALU.add)
                yield lambda: dve.scalar_tensor_tensor(out=slot_hi[:, :, T], in0=best_no[:, :, T], scalar=float(ST),
                                                       in1=slot_hi[:, :, T], op0=ALU.mult, op1=ALU.add)
                yield lambda: dve.tensor_tensor(slot_hi[:, :, T], slot_hi[:, :, T], away[:, :, T], ALU.add)

            def weigh_them():
                yield lambda: dve.tensor_scalar(gden[:, T], gexp[:, T], 1.0, None, ALU.add)
                yield lambda: dve.reciprocal(gate[:, 0, T], gden[:, T])
                yield lambda: dve.tensor_tensor(gate[:, 1, T], gexp[:, T], gate[:, 0, T], ALU.mult)
                yield lambda: dve.tensor_tensor(gate[:, :, T], gate[:, :, T], kept[:, :, T], ALU.mult)
                yield lambda: dve.tensor_tensor(gden[:, T], gate[:, 0, T], gate[:, 1, T], ALU.add)
                yield lambda: dve.tensor_scalar(gden[:, T], gden[:, T], 1e-9, None, ALU.add)
                yield lambda: dve.reciprocal(gden[:, T], gden[:, T])
                yield lambda: dve.tensor_scalar(gden[:, T], gden[:, T], tanh_g[:, 1:2], None, ALU.mult)
                yield lambda: dve.tensor_tensor(gate[:, :, T], gate[:, :, T],
                                                gden[:, T].rearrange("p (o t) -> p o t", o=1)
                                                .to_broadcast([P, TOPK, nt]), ALU.mult)

            carry = lambda: dve.tensor_copy(taken[:, 0, :], taken[:, nt, :])
            wait(dve, counted, odds, gates_read[0])
            yield from chained(route, place_them(), weigh_them())
            count_bank.free = (route, route.value)
            yield from chained(route, [carry])
            wait(dve, (route, route.value))
            routed = (route, route.value)
            for k in range(TOPK):
                for t0 in range(0, nt, TG):
                    i = groups_made[0] % len(at_lo)
                    groups_made[0] += 1
                    lo, eq, hi = at_lo[i], at_eq[i], at_hi[i]
                    tt = slice(t0, t0 + TG)

                    def per_tile(ap, n):
                        return ap.rearrange("p (t o) -> p t o", o=1).to_broadcast([P, TG, n])

                    def per_column(n):
                        return row_no[:, 0:n].rearrange("p (o r) -> p o r", o=1).to_broadcast([P, TG, n])

                    one = S("dve_one_hot")
                    while lo.free is None:
                        yield STUCK
                    wait(dve, eq.free)
                    eq_made = one.up(dve.tensor_tensor(eq.ap[:], per_column(NROW), per_tile(slot_hi[:, k, tt], NROW),
                                                       ALU.is_equal))
                    wait(pool, eq_made, routed, hi.free)
                    S("pool_table").up(pool.tensor_tensor(hi.ap[:, :, 0, :], eq.ap[:],
                                                          per_tile(token_no[:, v0 + t0:v0 + t0 + TG], NROW),
                                                          ALU.mult))
                    hi_made = eq.free = S("pool_table").up(pool.tensor_tensor(
                        hi.ap[:, :, 1, :], eq.ap[:], per_tile(gate[:, k, tt], NROW), ALU.mult))
                    gates_read[0] = hi_made
                    yield
                    wait(dve, lo.free)
                    lo_made = one.up(dve.tensor_tensor(lo.ap[:], per_column(P), per_tile(slot_lo[:, k, tt], P),
                                                       ALU.is_equal))
                    deferred.append(lambda args=(lo, hi, lo_made, hi_made): add_to_table(*args))
                    lo.free = None
                    yield

        def load_chunk(n):
            e, c = divmod(n, NC)
            for i, (buf, src) in enumerate(zip(w_raw[n % 2], (
                    w1[e].rearrange("(k p) f -> p k f", p=P)[:, :, c * BANK:(c + 1) * BANK],
                    w2[e].rearrange("(f p) d -> p f d", p=P)[:, c * CF:(c + 1) * CF, :]))):
                wait(sp, buf.free)
                buf.ready = S(f"load_w{i + 1}_{n % 2}").dma(sp.dma_start(buf.ap[:], src))

        for b in (*ao_hi, *ao_lo, *xn2, xn2T, logitT, *at_lo, *at_eq, *at_hi):
            b.free = (attn_done, b.free)
        for b in (*w_raw[0], *w_raw[1]):
            b.free = attn_done
        batches = []
        left = NS
        while left:
            n = 2 if left > 2 else 1
            batches.append((NS - left, n))
            left -= n
        batch_of = {s: (s0, n) for s0, n in batches for s in range(s0, s0 + n)}
        tasks = {}

        def at_unit(v, f, *args):
            tasks.setdefault(v, []).append((f, args))

        def start_chain(c):
            chains.insert(0, c)
            return c

        routing = [None]

        def start_routing(s0, n):
            routing[0] = start_chain(route_batch(s0 * TPS, n * TPS))

        def end_routing():
            if routing[0]:
                finish(routing[0])

        norming = {}

        def start_norm(s):
            norming[s] = start_chain(norm_steps(s))

        def end_norm(s):
            finish(norming[s], alone=s == NS - 1)
            norm_rows(s)
            if s == NS - 1:
                while chains and draw(1) is not STUCK:
                    pass
                emit_deferred()

        for s in range(NS):
            v = (s + 1) * TPS
            s0, n = batch_of[s]
            normed_at, turned_at, router_at, routed_at = ((0, 0, 0, 0) if s == NS - 1 else
                                                          (1, 2, 2, 3) if s == NS - 2 else (1, 2, 3, 4))
            at_unit(v + normed_at, end_norm, s)
            for k in range(KD):
                at_unit(v + turned_at, turn_rows_out, s, k)
            at_unit(v + router_at, router, s)
            v += routed_at
            if s == s0:
                at_unit(v, end_routing)
            at_unit(v, turn_logits, s, (s - s0) * TPS)
            if s == s0 + n - 1:
                at_unit(v, start_routing, s0, n)
        at_unit(NT - TPS - 3, load_chunk, 0)
        at_unit(NT - 3, load_chunk, 1)
        split_attn(0)
        split_attn(1)
        add_bo(0)
        add_bo(1)
        constants_done = late_constants()
        for v in range(NT + 1):
            if v < NT:
                bank = project_out(v)
                emit_deferred()
            draw(4)
            for f, args in tasks.get(v, ()):
                f(*args)
                draw(2)
            if v < NT:
                s, t = divmod(v, TPS)
                residual(v, bank)
                if t == TPS - 1:
                    start_norm(s)
                draw(4)
                if v + 2 < NT:
                    split_attn(v + 2)
                    add_bo(v + 2)
                draw(5)
        assert not [v for v in tasks if v > NT]
        end_routing()
        emit_deferred()

        S("act_gelu").up(act.activation(no_nan[:], no_nan[:], ACT.Gelu))
        out_written = (stored, stored.value)
        normed_written = tuple((q, q.value) for q in stored_norm)
        wait(dve, (S("pe_table"), S("pe_table").value))
        route.up(dve.tensor_copy(slot_gate[:], table_bank.ap[:, NROW:2 * NROW]))
        wait(dve, route.up(dve.tensor_scalar(empty[:], table_bank.ap[:, 0:NROW], 1.0, FAR, ALU.is_lt, ALU.mult)))
        table_done = route.up(dve.scalar_tensor_tensor(out=slot_token[:], in0=table_bank.ap[:, 0:NROW], scalar=-1.0,
                                                       in1=empty[:], op0=ALU.add, op1=ALU.add))
        wait(pe, (route, route.value), count_bank.free)
        summed = S("pe_count").up(pe.matmul(count_bank.ap[0:1, 0:E], ones_b[:, 0:1], taken[:, 0, :], start=True,
                                            stop=True))
        wait(dve, summed)
        choices_done = route.up(dve.tensor_copy(choices[:], count_bank.ap[0:1, 0:E]))
        count_bank.free = choices_done
        stage2_done = (choices_done, out_written, *normed_written)

        all_banks = [Buf(ring_a[0]), Buf(ring_a[1]), Buf(pair[0][:, 0, :]), Buf(pair[0][:, 1, :]),
                     Buf(pair[1][:, 0, :]), Buf(pair[1][:, 1, :]), Buf(ring_b[0]), Buf(ring_b[1])]
        for n, old in enumerate((bank_a[0], bank_a[1], logit_bank, logit_turn_bank, count_bank, table_bank,
                                 bank_b[0], bank_b[1])):
            all_banks[n].free = table_done if old is table_bank else old.free
        y_banks, m_banks = all_banks[1:1 + ST], [all_banks[0], *all_banks[1 + ST:]]

        wait(pool, attn_done)
        cleared = S("pool_clear").up(pool.memset(xg.ap[:], 0.0))
        wait(pool, cleared)

        fetched = {}

        def gather(e):
            wait(pool, table_done, *normed_written, xg.free)
            for t in range(ST):
                i = e * ST + t
                fetched[t] = S(f"gather{t}").dma(pool.indirect_dma_start(
                    xg.ap[:, t, :], None, normed, bass.IndirectOffsetOnAxis(ap=slot_token[:, i:i + 1], axis=0),
                    bounds_check=TOK - 1, oob_is_err=False))

        def load_b2(e):
            b = b2_rows[e % 2]
            wait(sp, b.free, stage2_done)
            b.ready = S(f"load_b2_{e % 2}").dma(sp.dma_start(b.ap[:], b2[e].partition_broadcast(P)))

        steps = {pe: [], act: [], dve: []}

        def step(eng, events, emit):
            news = unseen(eng, *events)

            def run(width):
                for sem, value in news:
                    eng.wait_ge(sem.sem, value)
                emit(width)
            steps[eng].append(run)

        def one_step(eng, name, events, emit):
            done = S(name).later()
            step(eng, events, lambda width: emit().then_inc(done[0].sem, 1))
            return done

        def play(eng, width):
            for run in steps[eng]:
                run(width)

        def play_by_count(eng, count, widths):
            if len(widths) == 1:
                play(eng, widths[0])
                return
            half = len(widths) // 2
            with eng.If(count <= widths[half - 1]):
                play_by_count(eng, count, widths[:half])
            with eng.Else():
                play_by_count(eng, count, widths[half:])

        def parts_of(width):
            return [(0, width)] if width <= BANK else [(0, FULL_RATE), (FULL_RATE, width)]

        def split_chunk(n, i, pieces):
            src, hi, lo = w_raw[n % 2][i], w_split[n % 2][2 * i], w_split[n % 2][2 * i + 1]
            for c in pieces:
                hi.ready = one_step(act, "act_whi", (src.ready, hi.free, stage2_done), lambda c=c: act.activation(
                    hi.ap[:, c, :], src.ap[:, c, :], ACT.Copy))
                lo.ready = one_step(dve, "dve_wlo", (src.ready, hi.ready, lo.free, stage2_done),
                                    lambda c=c: dve.tensor_tensor(lo.ap[:, c, :], src.ap[:, c, :], hi.ap[:, c, :],
                                                                  ALU.subtract))
            src.free = (hi.ready, lo.ready)

        turned_rows = {}

        def turn_rows(e, t, bank):
            hi_b, lo_b = xgT[e % 2]
            turned = S("pe_turn_g").later()

            def emit(width):
                for k in range(KD):
                    ins = pe.transpose(bank.ap[:, k * P:(k + 1) * P], xg.ap[:, t, k * P:(k + 1) * P], ident[:])
                ins.then_inc(turned[0].sem, 1)

            step(pe, (bank.free, fetched[t]), emit)
            sl = slice(t * P, (t + 1) * P)
            src = bank.ap[:, :].rearrange("p (k n) -> p k n", n=P)
            hi = one_step(act, "act_gT", (turned, hi_b.free, stage2_done),
                          lambda: act.activation(hi_b.ap[:, :, sl], src, ACT.Copy))
            lo = one_step(dve, "dve_gT", (turned, hi, lo_b.free, stage2_done),
                          lambda: dve.tensor_tensor(lo_b.ap[:, :, sl], src, hi_b.ap[:, :, sl], ALU.subtract))
            bank.free = (hi, lo)
            turned_rows[e, t] = (hi, lo)
            if t == ST - 1:
                xg.free = turned

        def hidden(e, f):
            q = e * NF + f
            n, j = divmod(q, CF)
            w_hi, w_lo = w_split[n % 2][0], w_split[n % 2][1]
            x_hi, x_lo = xgT[e % 2]
            c = slice(j * P, (j + 1) * P)
            banks = [take("m", m_banks) for _ in range(2)]
            hh, hl, hf = h_hi[q % NH], h_lo[q % NH], h_full[q % 2]
            bias = b1_cols[:, q:q + 1]
            done = [S("pe_hidden").later() for _ in range(2)]
            full, high, low = [], [], []
            for _ in range(2):
                full.append(S("act_gelu").later())
                high.append(S("act_gelu").later())
                low.append(S("dve_hlo").later())

            def multiply(i, width):
                parts = parts_of(width)
                if i < len(parts):
                    lo, hi = parts[i]
                    sl = slice(lo, hi)
                    ins = split_products(banks[i].ap[:, 0:hi - lo], range(KD), lambda k: w_hi.ap[:, k, c],
                                         lambda k: w_lo.ap[:, k, c], lambda k: x_hi.ap[:, k, sl],
                                         lambda k: x_lo.ap[:, k, sl])
                    ins.then_inc(done[i][0].sem, 3 - len(parts) if i == 0 else 1)

            def gelu(i, width):
                parts = parts_of(width)
                if i < len(parts):
                    lo, hi = parts[i]
                    src = banks[i].ap[:, 0:hi - lo]
                    act.activation(hf.ap[:, lo:hi], src, ACT.Gelu, bias=bias).then_inc(full[i][0].sem, 1)
                    act.activation(hh.ap[:, lo:hi], src, ACT.Gelu, bias=bias).then_inc(
                        high[i][0].sem, 3 if len(parts) == 1 else 1)

            def residue(i, width):
                parts = parts_of(width)
                if i < len(parts):
                    sl = slice(*parts[i])
                    dve.tensor_tensor(hl.ap[:, sl], hf.ap[:, sl], hh.ap[:, sl], ALU.subtract).then_inc(
                        low[i][0].sem, 3 - len(parts) if i == 0 else 1)

            for i in range(2):
                step(pe, (banks[i].free, [turned_rows[e, t] for t in range(ST)] if f or i else
                          [turned_rows[e, t] for t in range(-(-BANK // P))], w_hi.ready, w_lo.ready),
                     lambda width, i=i: multiply(i, width))
                step(act, (done[i], hf.free, hh.free, stage2_done), lambda width, i=i: gelu(i, width))
                step(dve, (full[i], high[i], hl.free, stage2_done), lambda width, i=i: residue(i, width))
                banks[i].free = high[i]
            hf.free = low[1]
            if j == CF - 1:
                w_hi.free = w_lo.free = done[1]
            if f == NF - 1:
                x_hi.free = x_lo.free = done[1]
            hh.ready, hl.ready = high[1], low[1]

        def start_y(e):
            b = b2_rows[e % 2]
            for t in range(ST):
                i = e * ST + t
                y.ready = one_step(dve, "dve_y", (b.ready, y.free, stage2_done), lambda t=t, i=i: dve.tensor_scalar(
                    y.ap[:, t, :], b.ap[:], slot_gate[:, i:i + 1], None, ALU.mult))
            b.free = y.ready

        def down(e, f):
            q = e * NF + f
            n, j = divmod(q, CF)
            w_hi, w_lo = w_split[n % 2][2], w_split[n % 2][3]
            hh, hl = h_hi[q % NH], h_lo[q % NH]
            done = [S("pe_down").later() for _ in (range(ST) if f == NF - 1 else range(1))]

            def emit(width):
                tiles = -(-width // P)
                for t in range(tiles):
                    sl = slice(t * P, min((t + 1) * P, width))
                    ins = split_products(y_banks[t].ap[0:sl.stop - sl.start, :], [j], lambda k: hh.ap[:, sl],
                                         lambda k: hl.ap[:, sl], lambda k: w_hi.ap[:, k, :],
                                         lambda k: w_lo.ap[:, k, :], first=f == 0, last=f == NF - 1)
                    if t == tiles - 1:
                        ins.then_inc(done[0][0].sem, len(done) if f < NF - 1 else ST - t)
                    elif f == NF - 1:
                        ins.then_inc(done[0][0].sem, 1)

            step(pe, [hh.ready, hl.ready, w_hi.ready, w_lo.ready] + ([b.free for b in y_banks] if f == 0 else []), emit)
            hh.free = hl.free = done[-1]
            if j == CF - 1:
                w_hi.free = w_lo.free = done[-1]
            if f == NF - 1:
                for t in range(ST):
                    finish_y(e, t, y_banks[t], done[t])

        def finish_y(e, t, bank, product):
            i = e * ST + t
            bank.free = one_step(dve, "dve_yout", (product, y.ready), lambda: dve.scalar_tensor_tensor(
                out=y.ap[:, t, :], in0=bank.ap[:, :], scalar=slot_gate[:, i:i + 1], in1=y.ap[:, t, :], op0=ALU.mult,
                op1=ALU.add))
            wait(pool, bank.free, out_written, landed[e - 1] if e else None)
            landed[e] = S("scatter_out").dma(pool.indirect_dma_start(
                out_rows, bass.IndirectOffsetOnAxis(ap=slot_token[:, i:i + 1], axis=0), y.ap[:, t, :], None,
                bounds_check=TOK - 1, oob_is_err=False, compute_op=ALU.add))
            y.free = landed[e]

        landed = {}
        LAG = 2
        gather(0)
        load_b2(0)
        split_chunk(0, 0, range(CF))
        for t in range(ST):
            turn_rows(0, t, y_banks[t])
        split_chunk(0, 1, range(CF))
        for eng in steps:
            play(eng, CAP)
        for e in range(E):
            for eng in steps:
                steps[eng].clear()
            for f in range(NF + LAG):
                q = e * NF + f
                n, j = divmod(q, CF)
                if f < NF:
                    if e + 1 < E:
                        if f == 2:
                            gather(e + 1)
                            load_b2(e + 1)
                        if 8 <= f < 8 + ST:
                            turn_rows(e + 1, f - 8, take("m", m_banks))
                    if f == 5:
                        start_y(e)
                    hidden(e, f)
                    if j == 0 and n + 2 < E * NC:
                        load_chunk(n + 2)
                    if n + 1 < E * NC:
                        half = j % (CF // 2) * (CF // 2)
                        split_chunk(n + 1, j // (CF // 2), range(half, half + CF // 2))
                if f >= LAG:
                    down(e, f - LAG)
            for eng in steps:
                wait(eng, choices_done)
                play_by_count(eng, eng.value_load(choices[0:1, e:e + 1]), WIDTHS)
        wait(sp, out_written, *normed_written, landed[E - 1])
        wait(pool, landed[E - 1])


_INS = ['x', 'ctx_768', 'g_xattn', 'g_ffn', 'L0_xattn_Wq', 'L0_xattn_bq', 'L0_xattn_Wk', 'L0_xattn_bk',
        'L0_xattn_Wv', 'L0_xattn_bv', 'L0_xattn_Wo', 'L0_xattn_bo', 'L0_ffn_router_w', 'L0_ffn_router_b',
        'L0_ffn_w1', 'L0_ffn_b1', 'L0_ffn_w2', 'L0_ffn_b2']
_OUTS = [((2, 2048, 512), 'float32')]


def kernel(**inputs):
    import numpy as _np
    import concourse.bacc as _bacc
    from concourse import mybir as _mybir
    from concourse.bass_utils import run_bass_kernel_spmd as _run

    nc = _bacc.Bacc("TRN2", target_bir_lowering=False, num_devices=1)
    arrays, args = {}, []
    for name in _INS:
        a = _np.ascontiguousarray(inputs[name])
        arrays[f"in_{name}_dram"] = a
        args.append(nc.dram_tensor(f"in_{name}_dram", a.shape, _mybir.dt.from_np(a.dtype), kind="ExternalInput").ap())
    for i, (shape, dtype) in enumerate(_OUTS):
        dt = _mybir.dt.from_np(_np.dtype(dtype))
        args.append(nc.dram_tensor(f"out_{i}_dram", shape, dt, kind="ExternalOutput").ap())
    moe_block_kernel(nc, *args)
    r = _run(nc, [arrays], core_ids=[0])
    got = tuple(r.results[0][f"out_{i}_dram"] for i in range(len(_OUTS)))
    return got[0]
```
